# Optimizing a Trainium2 kernel written in Bass

```python
import numpy as np
import jax
import jax.numpy as jnp

def _softmax(x, axis=-1):
    return jax.nn.softmax(x, axis=axis)

def _gelu(x):
    return jax.nn.gelu(x, approximate=True)

def _silu(x):
    return jax.nn.silu(x)

def _sigmoid(x):
    return jax.nn.sigmoid(x)

def _layernorm(x, axis=-1, eps=1e-05):
    m = jnp.mean(x, axis=axis, keepdims=True)
    v = jnp.var(x, axis=axis, keepdims=True)
    return (x - m) / jnp.sqrt(v + eps)

def _scatter_add(tgt, idx, src, axis=0):
    return tgt.at[idx].add(src)

def _segment_sum(src, seg, n):
    return jax.ops.segment_sum(src, seg, n)
kernel_name = 'mk_recurrent_d1_jaxref_r8_79795c'

def setup_inputs(seed: int=0):
    np.random.seed(seed)
    _w = jnp.asarray

    def _L0_attn_setup():
        import jax, jax.numpy as jnp
        import numpy as np
        from math import sqrt
        D_MODEL = 128
        NUM_HEADS = 16
        D_HEAD = D_MODEL // NUM_HEADS
        THETA = 10000.0

        def _rope(x, freqs):
            xr = x[..., ::2]
            xi = x[..., 1::2]
            cos = jnp.cos(freqs)
            sin = jnp.sin(freqs)
            yr = xr * cos - xi * sin
            yi = xr * sin + xi * cos
            return jnp.stack([yr, yi], axis=-1).reshape(x.shape)
        key = jax.random.key(seed)
        k1, k2, k3 = jax.random.split(key, 3)
        X = jax.random.normal(k1, (4, 256, D_MODEL), dtype=jnp.float32)
        std_kqv = sqrt(2.0 / (D_MODEL + 3 * D_MODEL))
        W_KQV = std_kqv * jax.random.truncated_normal(k2, -3.0, 3.0, (3 * D_MODEL, D_MODEL), dtype=jnp.float32)
        std_o = sqrt(2.0 / (D_MODEL + D_MODEL))
        W_O = std_o * jax.random.truncated_normal(k3, -3.0, 3.0, (D_MODEL, D_MODEL), dtype=jnp.float32)
        return {'X': X, 'W_KQV': W_KQV, 'W_O': W_O}
    _L0_attn_in = _L0_attn_setup()

    def _L0_ffn_setup():
        import jax, jax.numpy as jnp
        import numpy as np
        B, S, D = (1, 256, 128)
        I = 256
        E = 8
        K = 2
        LIMIT = 7.0
        ALPHA = 1.702
        EPS = 1e-05

        def _swiglu(h):
            x_glu = jnp.minimum(h[..., ::2], LIMIT)
            x_lin = jnp.clip(h[..., 1::2], -LIMIT, LIMIT)
            return x_glu * jax.nn.sigmoid(ALPHA * x_glu) * (x_lin + 1.0)

        def _moe(t, gate_w, gate_b, mlp1_w, mlp1_b, mlp2_w, mlp2_b):
            T = t.shape[0]
            logits = t @ gate_w + gate_b
            top_v, top_i = jax.lax.top_k(logits, K)
            probs = jax.nn.softmax(top_v, axis=-1)
            w = jnp.zeros((T, E), t.dtype).at[jnp.arange(T)[:, None], top_i].set(probs)

            def body(acc, ew):
                w1, b1, w2, b2, we = ew
                h = _swiglu(t @ w1 + b1)
                y = h @ w2 + b2
                return (acc + we[:, None] * y, None)
            acc0 = jnp.zeros((T, t.shape[1]), t.dtype)
            acc, _ = jax.lax.scan(body, acc0, (mlp1_w, mlp1_b, mlp2_w, mlp2_b, w.T))
            return acc
        key = jax.random.key(seed)
        ks = jax.random.split(key, 4)
        s = 0.02
        return {'x': jax.random.normal(ks[0], (B, S, D), jnp.float32), 'norm_scale': jnp.ones((D,), jnp.float32), 'gate_w': jax.random.normal(ks[1], (D, E), jnp.float32) * s, 'gate_b': jnp.zeros((E,), jnp.float32), 'mlp1_w': jax.random.normal(ks[2], (E, D, 2 * I), jnp.float32) * s, 'mlp1_b': jnp.zeros((E, 2 * I), jnp.float32), 'mlp2_w': jax.random.normal(ks[3], (E, I, D), jnp.float32) * s, 'mlp2_b': jnp.zeros((E, D), jnp.float32)}
    _L0_ffn_in = _L0_ffn_setup()
    _d = {'L0_attn_X': _L0_attn_in['X'], 'L0_attn_W_KQV': _L0_attn_in['W_KQV'], 'L0_attn_W_O': _L0_attn_in['W_O'], 'L0_ffn_norm_scale': _L0_ffn_in['norm_scale'], 'L0_ffn_gate_w': _L0_ffn_in['gate_w'], 'L0_ffn_gate_b': _L0_ffn_in['gate_b'], 'L0_ffn_mlp1_w': _L0_ffn_in['mlp1_w'], 'L0_ffn_mlp1_b': _L0_ffn_in['mlp1_b'], 'L0_ffn_mlp2_w': _L0_ffn_in['mlp2_w'], 'L0_ffn_mlp2_b': _L0_ffn_in['mlp2_b']}
    _x0 = _d['L0_attn_X']
    _d['L0_attn_X'] = jax.random.normal(jax.random.fold_in(jax.random.key(seed), 1), (8, 512, 128), dtype=_x0.dtype)
    del _x0
    return _d

def reference(L0_attn_X, L0_attn_W_KQV, L0_attn_W_O, L0_ffn_norm_scale, L0_ffn_gate_w, L0_ffn_gate_b, L0_ffn_mlp1_w, L0_ffn_mlp1_b, L0_ffn_mlp2_w, L0_ffn_mlp2_b):

    def _L0_attn_ref(X, W_KQV, W_O):
        import jax, jax.numpy as jnp
        import numpy as np
        from math import sqrt
        D_MODEL = 128
        NUM_HEADS = 16
        D_HEAD = D_MODEL // NUM_HEADS
        THETA = 10000.0

        def _rope(x, freqs):
            xr = x[..., ::2]
            xi = x[..., 1::2]
            cos = jnp.cos(freqs)
            sin = jnp.sin(freqs)
            yr = xr * cos - xi * sin
            yi = xr * sin + xi * cos
            return jnp.stack([yr, yi], axis=-1).reshape(x.shape)
        B, S, D = X.shape
        H, d = (NUM_HEADS, D_HEAD)
        KQV = jnp.einsum('bsd,ed->bse', X, W_KQV)
        K, Q, V = jnp.split(KQV, [D, 2 * D], axis=-1)

        def to_heads(t):
            return t.reshape(B, S, H, d).transpose(0, 2, 1, 3)
        K, Q, V = (to_heads(K), to_heads(Q), to_heads(V))
        inv_freq = 1.0 / THETA ** (jnp.arange(0, d, 2, dtype=jnp.float32) / d)
        pos = jnp.arange(S, dtype=jnp.float32)
        freqs = pos[:, None] * inv_freq[None, :]
        Q = _rope(Q, freqs)
        K = _rope(K, freqs)
        scores = jnp.einsum('bhqd,bhkd->bhqk', Q, K) / sqrt(d)
        causal = jnp.triu(jnp.ones((S, S), dtype=bool), k=1)
        scores = jnp.where(causal, -jnp.inf, scores)
        probs = jax.nn.softmax(scores, axis=-1)
        heads = jnp.einsum('bhqk,bhkd->bhqd', probs, V)
        acts = heads.transpose(0, 2, 1, 3).reshape(B, S, D)
        return jnp.einsum('bsd,ed->bse', acts, W_O)

    def _L0_ffn_ref(x, norm_scale, gate_w, gate_b, mlp1_w, mlp1_b, mlp2_w, mlp2_b):
        import jax, jax.numpy as jnp
        import numpy as np
        B, S, D = (1, 256, 128)
        I = 256
        E = 8
        K = 2
        LIMIT = 7.0
        ALPHA = 1.702
        EPS = 1e-05

        def _swiglu(h):
            x_glu = jnp.minimum(h[..., ::2], LIMIT)
            x_lin = jnp.clip(h[..., 1::2], -LIMIT, LIMIT)
            return x_glu * jax.nn.sigmoid(ALPHA * x_glu) * (x_lin + 1.0)

        def _moe(t, gate_w, gate_b, mlp1_w, mlp1_b, mlp2_w, mlp2_b):
            T = t.shape[0]
            logits = t @ gate_w + gate_b
            top_v, top_i = jax.lax.top_k(logits, K)
            probs = jax.nn.softmax(top_v, axis=-1)
            w = jnp.zeros((T, E), t.dtype).at[jnp.arange(T)[:, None], top_i].set(probs)

            def body(acc, ew):
                w1, b1, w2, b2, we = ew
                h = _swiglu(t @ w1 + b1)
                y = h @ w2 + b2
                return (acc + we[:, None] * y, None)
            acc0 = jnp.zeros((T, t.shape[1]), t.dtype)
            acc, _ = jax.lax.scan(body, acc0, (mlp1_w, mlp1_b, mlp2_w, mlp2_b, w.T))
            return acc
        Bx, Sx, Dx = x.shape
        ms = jnp.mean(x * x, axis=-1, keepdims=True)
        t = (x * jax.lax.rsqrt(ms + EPS) * norm_scale).reshape(Bx * Sx, Dx)
        y = _moe(t, gate_w, gate_b, mlp1_w, mlp1_b, mlp2_w, mlp2_b)
        return x + y.reshape(Bx, Sx, Dx)
    x = L0_attn_X
    xn = _layernorm(x, axis=-1)
    s = _L0_attn_ref(xn, L0_attn_W_KQV, L0_attn_W_O)
    g = _silu(_L0_ffn_ref(xn, L0_ffn_norm_scale, L0_ffn_gate_w, L0_ffn_gate_b, L0_ffn_mlp1_w, L0_ffn_mlp1_b, L0_ffn_mlp2_w, L0_ffn_mlp2_b))
    x = x + s * g
    return x

_drawn_inputs = setup_inputs


def setup_inputs(seed=0):
    import zlib

    import numpy as np

    out = dict(_drawn_inputs(seed))
    spreads = {'L0_ffn_norm_scale': (1.0, 0.6),
     'L0_ffn_gate_b': (0.0, 0.8),
     'L0_ffn_mlp1_b': (0.0, 0.8),
     'L0_ffn_mlp2_b': (0.0, 0.8)}
    factors = {'L0_ffn_gate_w': 8.0, 'L0_ffn_mlp1_w': 8.0, 'L0_ffn_mlp2_w': 8.0}
    for name, (base, spread) in spreads.items():
        noise = np.random.default_rng([zlib.crc32(name.encode()), seed]).standard_normal(out[name].shape)
        drawn = base * np.exp(spread * noise) if base else spread * noise
        out[name] = jnp.asarray(drawn.astype(out[name].dtype))
    for name, factor in factors.items():
        out[name] = (out[name] * factor).astype(out[name].dtype)
    return out
```

```python
from contextlib import ExitStack

import numpy as np

import concourse.bass as bass
from concourse import mybir

F32 = mybir.dt.float32
BF16 = mybir.dt.bfloat16
I32 = mybir.dt.int32
U32 = mybir.dt.uint32
ALU = mybir.AluOpType
ACT = mybir.ActivationFunctionType
AX = mybir.AxisListType

P = 128
B, S, D = 8, 512, 128
H, DH = 16, 8
E, I = 8, 256
NQ = S // P
NT = B * NQ
HG = 4
NG = H // HG
HALF = H // 2
VC = 16
LIMIT, ALPHA, EPS, THETA = 7.0, 1.702, 1e-5, 10000.0
MASKED = -1e30

K_PART = (0, 0, 0, 1, 1, 2)
Q_PART = (0, 1, 2, 0, 1, 0)
MROW = 96

PT_AT = (0, 640, 1024, 512)
PT_COLS = 1280
UNITS = 5
STEPS = UNITS * H // 2

NF = (B * S * 2) // P + E
TILES_PER = (0, 12, 15, 15, 15, 15, 0, 0, 0)
assert sum(TILES_PER) == NF
FIRST, LOOPED, LAST = -2, (2, 5), B
SLOTS = 4


SELECTS = 3


def every_512(head):
    return bass.AP(
        tensor=head.tensor, offset=head.offset, ap=[head.ap[0], [512, 3], [1, P]])


def tiles_of(i):
    return TILES_PER[i] if i >= 0 else 0


def plan(i):
    at = [[] for _ in range(STEPS)]
    attend, score = 0 <= i < B, -1 <= i < B - 1
    project = -2 <= i < B - 2
    if attend:
        at[0].append(("msplit", 1))
        at[1].append(("mT", 1))
    if 1 <= i:
        at[2].append(("pv", 3))
        at[3].append(("oc", 3))
        at[4].append(("OT", 3))
        at[6].append(("AT", 0))
        at[7].append(("WO", 0))
    if attend:
        at[5].append(("V", 0))
        for g in range(3):
            at[10 * g + 12].append(("pv", g))
            at[10 * g + 13].append(("oc", g))
            at[10 * g + 14].append(("OT", g))
        for j in range(H // 2):
            at[min(5 * j + 5, STEPS - 1)].append(("sel", j))
    if project:
        for c in range(4):
            at[7 + c].append(("Q", c))
        at[11].append(("sum", 0))
        at[13].append(("hi", 0))
        at[14].append(("rest", 0))
        at[16].append(("mid", 0))
        at[17].append(("low", 0))
        at[18].append(("parts", 0))
        at[21].append(("stack", 0))
        at[39].append(("stack", 1))
    if score:
        at[20].append(("msplit", 0))
        at[21].append(("mT", 0))
    if -2 <= i <= 0:
        n = {-2: (0, 16), -1: (16, 40), 0: (40, 64)}[i]
        for m, t in enumerate(range(*n)):
            at[min(39, 15 + m)].append(("scatter", t))
    nf = tiles_of(i)
    for t in range(nf):
        s = 2 + (t * 33) // nf
        at[max(0, s - 2)].append(("xload", t))
        at[s].append(("xT", t))
        at[s + 1].append(("H", t))
        at[s + 2].append(("tanh", t))
        at[s + 3].append(("glu", t))
        at[s + 4].append(("hT", t))
        at[min(39, s + 5)].append(("y", t))
    if i in (6, 7):
        for n in range(4):
            c = 4 * (i - 6) + n
            for r in range(8):
                at[10 * n + r].append(("gather", (c, r)))
            if c < B - 1:
                at[10 * n + 9].append(("mix", c))
    if i == B:
        at[9].append(("mix", B - 1))
    return at


RING = ("Q", "V", "xT", "H", "hT", "y", "OT", "mT", "AT", "WO")
NAMES = ("msplit", "pv", "oc", "sel", "sum", "hi", "rest", "mid", "low", "parts", "scatter",
         "xload", "tanh", "glu", "gather", "mix", "st", "s", "group") + RING
NAMES += tuple(f"tile{s}" for s in range(SLOTS)) + ("stack0", "stack1", "mT0", "mT1")


def tally():
    before = {n: {FIRST: 0} for n in NAMES}
    for i in range(FIRST, LAST + 1):
        got = dict.fromkeys(NAMES, 0)
        for step in plan(i):
            for name, which in step:
                if name in got:
                    got[name] += 1
                if name in ("stack", "mT"):
                    got[f"{name}{which}"] += 1
        got["st"] = STEPS if 0 <= i < B else 0
        got["group"] = NG if 0 <= i < B else 0
        got["s"] = STEPS if -1 <= i < B - 1 else 0
        for s in range(SLOTS):
            got[f"tile{s}"] = len(range(s, tiles_of(i), SLOTS))
        for n in NAMES:
            before[n][i + 1] = before[n][i] + got[n]
    return before


BEFORE = tally()


class Iteration:

    def __init__(self, i, trip=None, times=None):
        self.i, self.trip = i, trip
        self.times = times
        self.attend, self.score = 0 <= i < B, -1 <= i < B - 1
        self.plan = plan(i)

    def seen(self, name, here=0):
        n = BEFORE[name][self.i] + here
        per = BEFORE[name][LOOPED[0] + 1] - BEFORE[name][LOOPED[0]]
        return n if self.trip is None or not per else self.times(2 * per) + n

    def batch(self, ahead=0):
        return self.i + ahead if self.trip is None else self.times(2) + (self.i + ahead)

    def tile(self, t):
        n = sum(TILES_PER[:max(self.i, 0)]) + t
        return n if self.trip is None else self.times(2 * TILES_PER[LOOPED[0]]) + n

    def ring(self):
        out, got = [], dict.fromkeys(RING, 0)
        for step in self.plan:
            for name, which in step:
                if name in RING:
                    out.append((name, which, got[name]))
                    got[name] += 1
        return out


def ring_of(it, name, a):
    for r, (n, w, _) in enumerate(it.ring()):
        if (n, w) == (name, a):
            return r

def mt_seen(it, f):
    return it.seen("mT", 0 if f or not it.attend else 1)


def atleast(eng, sem, n, each=1):
    if isinstance(n, int):
        if n > 0:
            eng.wait_ge(sem, n * each)
    else:
        eng.wait_ge(sem, n * each if each > 1 else n)


def run_iterations(eng, body):
    for i in range(FIRST, LOOPED[0]):
        body(Iteration(i))
    with eng.Fori(0, (LOOPED[1] - LOOPED[0] + 1) // 2) as trip:
        held = {}

        def times(k):
            if k not in held:
                held[k] = eng.snap(trip * k)
            return held[k]
        for i in (LOOPED[0], LOOPED[0] + 1):
            body(Iteration(i, trip, times))
    for i in range(LOOPED[1] + 1, LAST + 1):
        body(Iteration(i))


def build(nc, x_h, wq_h, wv_h, wo_h, cos_h, sin_h, scale_h, gate_w_h, gate_b_h, w1_h, b1_h, w2_h, b2_h, out_h):
    ctx = ExitStack()
    with ctx:
        def sb(name, shape, dt=F32):
            return ctx.enter_context(nc.sbuf_tensor(name, shape, dt))

        def sem(name):
            return ctx.enter_context(nc.semaphore(name))

        w1 = sb("w1", [P, E * 2 * I])
        w2 = sb("w2", [P, E * 2 * D])
        bias = sb("bias", [3, E * 2 * I + E * D], BF16)
        wq, wv, wo = sb("wq", [P, 4 * P]), sb("wv", [P, D]), sb("wo", [P, D])
        cos, sin = sb("cos", [P, S]), sb("sin", [P, S])
        xall = sb("xall", [P, NT, D])
        qs = [sb(f"qs{n}", [P, H, S], BF16) for n in range(2)]
        ks = [sb(f"ks{n}", [P, H, S], BF16) for n in range(2)]
        probs = sb("probs", [P, 2, HG, PT_COLS])
        vs = sb("vs", [P, NQ, H, VC])
        o_sb, acts, actsT = (sb(n, [P, S]) for n in ("o_sb", "acts", "actsT"))
        s_sb = acts
        qk = sb("qk", [P, 2, S])
        qk_sin = sb("qk_sin", [P, 2, S])
        parts = sb("parts", [P, 2, 3, S], BF16)
        xp = sb("xp", [P, S])
        xs = sb("xs", [P, SLOTS, D])
        xsT = sb("xsT", [P, 2, P])
        glu, lin, tanh_g = (sb(n, [P, 2, I]) for n in ("glu", "lin", "tanh_g"))
        hid = lin
        hidT = sb("hidT", [P, 2, 2, P])
        ys = sb("ys", [P, SLOTS, D])
        rowmax = sb("rowmax", [P, NQ, H])
        msplit = sb("msplit", [P, 2, NQ, 3, HALF], BF16)
        mrest = sb("mrest", [P, NQ, HALF])
        mT = sb("mT", [3 * HALF, 2, S], BF16)
        recip = sb("recip", [P, NQ, HG])
        ident, identb = sb("ident", [P, P]), sb("identb", [P, P], BF16)
        mask2 = sb("mask2", [P, 2, P], BF16)
        ones3 = sb("ones3", [3, P], BF16)
        ltri, onesb = sb("ltri", [P, P], BF16), sb("onesb", [P, P], BF16)
        scale, gate = sb("scale", [P, 1]), sb("gate", [P, E])
        gate_b = sb("gate_b", [P, E])
        stats, mv = sb("stats", [P, NT, 6]), sb("mv", [P, NT, 2])
        rs, rr, rt = sb("rs", [P, NT]), sb("rr", [P, NT]), sb("rt", [P, NT])
        sq, va = sb("sq", [P, NT]), sb("va", [P, NT])
        bparts = sb("bparts", [P, 3, 40], BF16)
        braw = sb("braw", [P, 40])
        wts = sb("wts", [P, 2, NT])
        index = sb("index", [P, 2, NT], U32)
        expert = sb("expert", [1, NF], I32)

        bank = ctx.enter_context(nc.psum_tensor("bank", [P, 8, 512], F32))
        ST_BANK, S_BANK, PV_BANK, RING_BANK = (0, 1), (2, 3), 4, (5, 6, 7)

        NE = NT * E
        lg, oh1, oh2, sc1, sc2, posb = (t[:, n, :] for t in (glu, lin, tanh_g) for n in range(2))
        tot, inc, cmpj = (actsT[:, 0:NE], actsT[:, NE:2 * NE], acts[:, 0:NE])
        cbf = acts[:, NE:NE + NE // 2].bitcast(BF16)
        small = hidT[:, :, :, :].rearrange("p a b c -> p (a b c)")
        desc, jot, onef, v1, v2, nte, cn, e2, p1, idf = (small[:, NT * n:NT * (n + 1)] for n in range(10))
        desc = desc[:, 0:E]
        tio = small[:, NT * 10:NT * 10 + NF]
        ecmp = qk_sin[:, :, :].rearrange("p a b -> p (a b)")[:, 0:NF * E]
        esum, start8 = o_sb[:, 0:NF], o_sb[:, P:P + E]

        def cbuf(n):
            return xall[:, NQ * n:NQ * (n + 1), :]
        y_in = [[cbuf(0), cbuf(1)], [cbuf(2), cbuf(3)]]
        x_c, xn_c, s_c, t_c = cbuf(4), cbuf(5), cbuf(6), cbuf(7)

        def dram(name, shape, dt=F32):
            return nc.dram_tensor(name, shape, dt).ap()
        xnT_d = dram("xnT_d", (P, B * S))
        xn_d = dram("xn_d", (B * S, D))
        s_d = dram("s_d", (B * S, D))
        sorted_d = dram("sorted_d", (NF * P, D))
        y_d = dram("y_d", (NF * P, D))
        parts_d = dram("parts_d", (2, 2, 3, DH, H * S), BF16)
        m_d = dram("m_d", (2, 3, HALF * S), BF16)
        bias_d = dram("bias_d", (3, E * 2 * I + E * D), BF16)

        (weights_in, consts_made, zeroed, zero_rows, xn_out, xnT_out, bias_out, bias_in,
         scattered, routed) = (sem(n) for n in (
             "weights_in", "consts_made", "zeroed", "zero_rows", "xn_out", "xnT_out", "bias_out", "bias_in",
             "scattered", "routed"))
        x_in = [sem(f"x_in{n}") for n in range(B)]
        r_dve, r_act, r_pe = sem("r_dve"), sem("r_act"), sem("r_pe")
        rows_ready = sem("rows_ready")
        st_ready, exp_done, s_ready, max_done = (sem(n) for n in ("st_ready", "exp_done", "s_ready", "max_done"))
        selected, pv_done, o_copied, acts_done = (sem(n) for n in ("selected", "pv_done", "o_copied", "acts_done"))
        pair_seen = sem("pair_seen")
        recip_done, pv_zeroed = sem("recip_done"), sem("pv_zeroed")
        split_done, m_written = sem("split_done"), [sem(f"m_written{n}") for n in range(2)]
        m_in = [sem(f"m_in{n}") for n in range(2)]
        stack_in = [sem(f"stack_in{n}") for n in range(2)]
        xq_in, xv_in = sem("xq_in"), sem("xv_in")
        roped, qk_sum, hi_done, rest_done, mid_done, low_done, parts_out = (sem(n) for n in (
            "roped", "qk_sum", "hi_done", "rest_done", "mid_done", "low_done", "parts_out"))
        pe_done = {n: sem(f"{n}_ready") for n in RING}
        mT_copied, v_copied, aT_copied, s_copied, s_out = (sem(n) for n in (
            "mT_copied", "v_copied", "aT_copied", "s_copied", "s_out"))
        xs_in = [sem(f"xs_in{n}") for n in range(SLOTS)]
        y_out = [sem(f"y_out{n}") for n in range(SLOTS)]
        xsT_copied, halves_read, tanh_done, prod_done, hid_done, hidT_copied, y_copied = (sem(n) for n in (
            "xsT_copied", "halves_read", "tanh_done", "prod_done", "hid_done", "hidT_copied", "y_copied"))
        c_in, gathered, mix_step, mix_tanh, out_done = (sem(n) for n in (
            "c_in", "gathered", "mix_step", "mix_tanh", "out_done"))
        gathered = [sem("gathered0"), sem("gathered1")]

        reader = {"Q": (roped, 1), "V": (v_copied, 1), "xT": (xsT_copied, 1), "H": (halves_read, 2),
                  "hT": (hidT_copied, 1), "y": (y_copied, 1), "OT": (acts_done, 1), "mT": (mT_copied, 1),
                  "AT": (aT_copied, 1), "WO": (s_copied, 1)}

        W_LOADS = 12
        MIX = 7
        block = ctx.enter_context(nc.Block())

        @block.sync
        def _(sp):
            x_rows = x_h.rearrange("(b t p) d -> b p t d", p=P, t=NQ)
            xn_rows = xn_d.rearrange("(b t p) d -> b p t d", p=P, t=NQ)
            s_rows = s_d.rearrange("(b t p) d -> b p t d", p=P, t=NQ)
            out_rows = out_h.rearrange("(b t p) d -> b p t d", p=P, t=NQ)
            for b in range(B):
                sp.dma_start(xall[:, NQ * b:NQ * (b + 1), :], x_rows[b]).then_inc(x_in[b], 16)
            for dst, src in ((wq[:, :], wq_h), (wv[:, :], wv_h), (wo[:, :], wo_h), (cos[:, :], cos_h),
                             (sin[:, :], sin_h), (scale[:, :], scale_h), (gate[:, :], gate_w_h),
                             (gate_b[:, :], gate_b_h.partition_broadcast(P).rearrange("p a e -> p (a e)")), (w1[:, :], w1_h),
                             (w2[:, :], w2_h), (braw[:, 0:32], b1_h), (braw[:, 32:40], b2_h)):
                sp.dma_start(dst, src).then_inc(weights_in, 16)
            sp.wait_ge(zeroed, 1)
            zero = probs[:, 1, 0:2, :].rearrange("p a b -> p (a b)")[:, 0:NF * D // 4]
            z_d = sorted_d.rearrange("(p q r) d -> q p (r d)", p=P, q=4)
            for q in range(4):
                sp.dma_start(z_d[q], zero).then_inc(zero_rows, 16)
            sp.wait_ge(r_dve, 5)
            sp.dma_start(bias_d[:, 0:E * 2 * I].rearrange("c (p j) -> p c j", p=P), bparts[:, :, 0:32]).then_inc(bias_out, 16)
            sp.dma_start(bias_d[:, E * 2 * I:].rearrange("c (p j) -> p c j", p=P), bparts[:, :, 32:40]).then_inc(bias_out, 16)
            sp.wait_ge(bias_out, 32)
            sp.dma_start(bias[:, :], bias_d).then_inc(bias_in, 16)
            xnT = probs[:, 0, :, :].rearrange("p a b -> p (a b)")
            for b in range(B):
                sp.wait_ge(rows_ready, NQ * (b + 1))
                sp.dma_start(xn_rows[b], xall[:, NQ * b:NQ * (b + 1), :]).then_inc(xn_out, 16)
                sp.wait_ge(r_act, R_ACT_T + b + 1)
                sp.dma_start(xnT_d[:, b * S:(b + 1) * S], xnT[:, b * S:(b + 1) * S]).then_inc(xnT_out, 16)
            sp.wait_ge(xnT_out, 16 * B)

            def body(it):
                for k in range(STEPS):
                    if k == 3 and it.i >= 0 and it.attend:
                        atleast(sp, pe_done["Q"], it.seen("Q"))
                        sp.dma_start(xp[:, :], xnT_d[:, bass.ds(it.batch() * S, S)]).then_inc(xv_in, 16)
                    if k == 6 and it.i < B - 2:
                        atleast(sp, pe_done["Q"], it.seen("Q"))
                        if it.attend:
                            sp.wait_ge(pe_done["V"], it.seen("V", 1))
                        sp.dma_start(xp[:, :], xnT_d[:, bass.ds(it.batch(2) * S, S)]).then_inc(xq_in, 16)
                    for f, kw, ahead in ((1, 2, 0), (0, 22, 1)):
                        if k == kw and (it.attend if f else it.score):
                            sp.wait_ge(mT_copied, it.seen("mT", 1 if f or not it.attend else 2))
                            atleast(sp, m_in[f], it.seen(f"mT{f}"), 16)
                            sp.dma_start(m_d[f].rearrange("c (h q) -> (c h) q", h=HALF), mT[:, f, :]).then_inc(m_written[f], 16)
                        if k == kw + 2 and (it.attend if f else it.score):
                            n = it.seen(f"mT{f}", 1)
                            atleast(sp, m_written[f], n, 16)
                            par = (it.i + ahead) % 2
                            sp.dma_start(qs[par][MROW:MROW + 3, f * HALF:(f + 1) * HALF, :], m_d[f]).then_inc(m_in[f], 16)
                    for name, a in it.plan[k]:
                        if name == "parts":
                            sp.wait_ge(low_done, it.seen("low", 1))
                            for f in range(2):
                                atleast(sp, stack_in[f], it.seen(f"stack{f}"), 16 * 9)
                            sp.dma_start(parts_d[it.i % 2].rearrange("a c d (h q) -> (d h) (a c) q", h=H),
                                         parts[:, :, :, :].rearrange("p a c q -> p (a c) q")).then_inc(parts_out, 16)
                        elif name == "stack":
                            atleast(sp, parts_out, it.seen("parts", 1), 16)
                            if it.attend:
                                sp.wait_ge(st_ready, it.seen("st", 20 * (a + 1)))
                            src = parts_d[it.i % 2]
                            h0 = a * HALF
                            for t, row, qk_at, lo, n in [(qs, 0, 0, 0, 3), (qs, 24, 0, 0, 2), (qs, 40, 0, 0, 1)] + \
                                    [(ks, 8 * r, 1, part, 1) for r, part in enumerate(K_PART)]:
                                sp.dma_start(t[it.i % 2][row:row + DH * n, h0:h0 + HALF, :],
                                             src[qk_at, lo:lo + n, :, h0 * S:(h0 + HALF) * S].rearrange("c d x -> (c d) x")
                                             ).then_inc(stack_in[a], 16)
                        elif name == "xload":
                            s = a % SLOTS
                            if it.i == 1 and a == 0:
                                sp.wait_ge(scattered, 16 * 2 * NT)
                            if a < SLOTS:
                                atleast(sp, pe_done["xT"], it.seen("xT"))
                            else:
                                atleast(sp, pe_done["xT"], it.seen("xT", a - SLOTS + 1))
                            sp.dma_start(xs[:, s, :], sorted_d[bass.ds(it.tile(a) * P, P), :]).then_inc(xs_in[s], 16)
                        elif name == "y":
                            s = a % SLOTS
                            sp.wait_ge(y_copied, it.seen("y", a + 1))
                            sp.dma_start(y_d[bass.ds(it.tile(a) * P, P), :], ys[:, s, :]).then_inc(y_out[s], 16)
                        elif name == "WO":
                            sp.wait_ge(s_copied, it.seen("WO", 1))
                            sp.dma_start(s_d[bass.ds(it.batch(-1) * S, S), :].rearrange("(t p) d -> p t d", p=P),
                                         s_sb[:, :].rearrange("p (t d) -> p t d", t=NQ)).then_inc(s_out, 16)
                        elif name == "mix":
                            atleast(sp, out_done, a, 16)
                            atleast(sp, s_out, a + 1, 16)
                            sp.dma_start(x_c, x_rows[a]).then_inc(c_in, 16)
                            sp.dma_start(xn_c, xn_rows[a]).then_inc(c_in, 16)
                            sp.dma_start(s_c, s_rows[a]).then_inc(c_in, 16)
                            sp.wait_ge(mix_step, MIX * (a + 1))
                            sp.dma_start(out_rows[a], t_c).then_inc(out_done, 16)
            run_iterations(sp, body)
            sp.wait_ge(out_done, 16 * B)
            sp.wait_ge(xn_out, 16 * B)
            for s in range(SLOTS):
                sp.wait_ge(y_out[s], 16 * BEFORE[f"tile{s}"][LAST + 1])

        @block.gpsimd
        def _(pool):
            n_made = [0]

            def made(ins):
                n_made[0] += 1
                ins.then_inc(consts_made, 1)
                return n_made[0]

            nc.gpsimd.memset(probs[:, 1, 0:2, :], 0.0).then_inc(zeroed, 1)
            a = made(nc.gpsimd.memset(ident[:, :], 0.0))
            made(nc.gpsimd.memset(mask2[:, :, :], 0.0))
            made(nc.gpsimd.memset(ltri[:, :], 1.0))
            made(nc.gpsimd.memset(onesb[:, :], 1.0))
            b = made(nc.gpsimd.memset(ones3[:, :], 1.0))
            pool.wait_ge(consts_made, b)
            a = made(nc.gpsimd.affine_select(out=ident[:, :], in_=ident[:, :], compare_op=ALU.not_equal, fill=1.0,
                                             base=0, pattern=[[-1, P]], channel_multiplier=1))
            made(nc.gpsimd.affine_select(out=mask2[:, :, :], in_=mask2[:, :, :], compare_op=ALU.is_ge, fill=MASKED,
                                         base=0, pattern=[[0, 2], [-1, P]], channel_multiplier=1))
            made(nc.gpsimd.affine_select(out=ltri[:, :], in_=ltri[:, :], compare_op=ALU.is_gt, fill=0.0,
                                         base=0, pattern=[[1, P]], channel_multiplier=-1))
            pool.wait_ge(consts_made, a)
            made(nc.gpsimd.tensor_copy(identb[:, :], ident[:, :]))
            made(nc.gpsimd.iota(desc, pattern=[[-1, E]], base=E, channel_multiplier=0, allow_small_or_imprecise_dtypes=True))
            made(nc.gpsimd.iota(jot, pattern=[[P, NT]], base=0, channel_multiplier=0, allow_small_or_imprecise_dtypes=True))
            made(nc.gpsimd.iota(tio, pattern=[[1, NF]], base=0, channel_multiplier=0, allow_small_or_imprecise_dtypes=True))
            made(nc.gpsimd.memset(onef, 1.0))
            for par in range(2):
                made(nc.gpsimd.memset(qs[par][:, :, :], 0.0))
                made(nc.gpsimd.memset(ks[par][:, :, :], 0.0))
            a = made(nc.gpsimd.memset(vs[:, :, :, :], 0.0))
            pool.wait_ge(consts_made, a)
            for par in range(2):
                a = made(nc.gpsimd.memset(ks[par][MROW:P, :, :], 1.0))
            pool.wait_ge(consts_made, a)
            made(nc.gpsimd.memset(vs[:, :, :, DH:DH + 1], 1.0))
            assert n_made[0] == CONSTS

            def body(it):
                for k in range(STEPS):
                    for name, a in it.plan[k]:
                        if name == "sel":
                            pool.wait_ge(exp_done, it.seen("st", UNITS * (a + 1)))
                            pool.sem_inc(pair_seen, 1)
                            h0 = 2 * a % HG
                            heads = probs[:, a // 2 % 2, h0:h0 + 2, :]
                            for blk in (every_512(heads[:, 0, :]), every_512(heads[:, 1, :]), heads[:, :, PT_AT[1]:PT_AT[1] + P]):
                                nc.gpsimd.affine_select(out=blk, in_=blk, compare_op=ALU.is_ge, fill=0.0, base=0,
                                                        pattern=[[0, blk.shape[1]], [1, P]],
                                                        channel_multiplier=-1).then_inc(selected, 1)
                        elif name == "sum":
                            pool.wait_ge(roped, it.seen("Q", 4))
                            nc.gpsimd.tensor_tensor(qk[:, :, :], qk[:, :, :], qk_sin[:, :, :], ALU.add).then_inc(qk_sum, 1)
                        elif name == "rest":
                            pool.wait_ge(hi_done, it.seen("hi", 1))
                            nc.gpsimd.tensor_tensor(qk[:, :, :], qk[:, :, :], parts[:, :, 0, :], ALU.subtract).then_inc(rest_done, 1)
                        elif name == "low":
                            pool.wait_ge(mid_done, it.seen("mid", 1))
                            nc.gpsimd.tensor_tensor(parts[:, :, 2, :], qk[:, :, :], parts[:, :, 1, :], ALU.subtract).then_inc(low_done, 1)
                        elif name == "scatter":
                            if a == 0:
                                pool.wait_ge(routed, 1)
                                pool.wait_ge(zero_rows, 64)
                            s, t = a % 2, a // 2
                            nc.gpsimd.indirect_dma_start(
                                out=sorted_d, out_offset=bass.IndirectOffsetOnAxis(ap=index[:, s, t:t + 1], axis=0),
                                in_=xall[:, t, :], in_offset=None).then_inc(scattered, 16)
                        elif name == "gather":
                            c, r = a
                            if c == 0 and r == 0:
                                pool.wait_ge(scattered, 16 * 2 * NT)
                                for s in range(SLOTS):
                                    pool.wait_ge(y_out[s], 16 * BEFORE[f"tile{s}"][LAST + 1])
                            if r == 0 and c >= 2:
                                pool.wait_ge(mix_step, MIX * (c - 1))
                            s, t = r // NQ, r % NQ
                            nc.gpsimd.indirect_dma_start(
                                out=y_in[c % 2][s][:, t, :], out_offset=None, in_=y_d,
                                in_offset=bass.IndirectOffsetOnAxis(ap=index[:, s, NQ * c + t:NQ * c + t + 1], axis=0)
                                ).then_inc(gathered[c % 2], 16)
            run_iterations(pool, body)

        @block.scalar
        def _(act):
            act.wait_ge(r_dve, R_VAR)
            nc.scalar.activation(sq[:, :], va[:, :], ACT.Sqrt).then_inc(r_act, 1)
            act.wait_ge(r_dve, R_MS)
            nc.scalar.activation(sq[:, :], va[:, :], ACT.Sqrt).then_inc(r_act, 1)
            assert R_ACT_T == 2
            xnT = probs[:, 0, :, :].rearrange("p a b -> p (a b)")
            for b in range(B):
                act.wait_ge(r_pe, b + 1)
                nc.scalar.copy(xnT[:, b * S:(b + 1) * S], bank[:, b % 4, :]).then_inc(r_act, 1)
            act.wait_ge(r_pe, B)
            act.wait_ge(xn_out, 16 * B)
            act.wait_ge(r_dve, R_RR)
            for t in range(NT):
                ins = nc.scalar.mul(xall[:, t, :], xall[:, t, :], rr[:, t:t + 1])
            ins.then_inc(r_act, 1)
            act.wait_ge(r_dve, R_TOP)
            nc.scalar.activation(e2, e2, ACT.Exp).then_inc(r_act, 1)

            def body(it):
                y_seen = 0
                for k in range(STEPS):
                    if it.attend:
                        u, j = k % UNITS, k // UNITS
                        g, h0 = j // 2, 2 * j % HG
                        act.wait_ge(st_ready, it.seen("st", k + 1))
                        if it.i == 0 and k == 0:
                            act.wait_ge(xnT_out, 16 * B)
                            act.wait_ge(zero_rows, 64)
                        if j % 2 == 0 and u == 0:
                            atleast(act, pv_done, it.seen("group", g - 1))
                        pt = probs[:, g % 2, :, :]
                        src = bank[:, ST_BANK[k % 2], :]
                        if u == 4:
                            dst = pt[:, h0:h0 + 2, PT_AT[2]:PT_AT[2] + 256]
                            src = src.rearrange("p (h q) -> p h q", h=2)
                        else:
                            lo = 512 * (u % 2)
                            dst = pt[:, h0 + u // 2, lo:lo + 512]
                        nc.scalar.activation(dst, src, ACT.Exp, scale=float(DH) ** -0.5).then_inc(exp_done, 1)
                    for name, a in it.plan[k]:
                        if name in RING:
                            r = ring_of(it, name, a)
                            src = bank[:, RING_BANK[r % 3], :]
                        if name == "oc":
                            n = it.seen("oc", (a + 1) % 4 if it.i >= 1 else a)
                            act.wait_ge(pv_done, n + 1)
                            atleast(act, pe_done["OT"], n)
                            nc.scalar.copy(o_sb[:, :], bank[:, PV_BANK, :]).then_inc(o_copied, 1)
                        elif name == "V":
                            act.wait_ge(pe_done["V"], it.seen("V", 1))
                            atleast(act, pv_done, it.seen("group"))
                            if it.i == 0:
                                act.wait_ge(consts_made, CONSTS)
                            nc.scalar.copy(vs[:, :, :, 0:DH], src.rearrange("p (k h d) -> p k h d", k=NQ, h=H)).then_inc(v_copied, 1)
                        elif name == "mT":
                            act.wait_ge(pe_done["mT"], mt_seen(it, a) + 1)
                            atleast(act, m_written[a], it.seen(f"mT{a}"), 16)
                            nc.scalar.copy(mT[:, a, :], bank[0:3 * HALF, RING_BANK[r % 3], 0:256].bitcast(BF16)).then_inc(mT_copied, 1)
                        elif name == "hi":
                            act.wait_ge(qk_sum, it.seen("sum", 1))
                            atleast(act, parts_out, it.seen("parts"), 16)
                            nc.scalar.copy(parts[:, :, 0, :], qk[:, :, :]).then_inc(hi_done, 1)
                        elif name == "mid":
                            act.wait_ge(rest_done, it.seen("rest", 1))
                            nc.scalar.copy(parts[:, :, 1, :], qk[:, :, :]).then_inc(mid_done, 1)
                        elif name == "AT":
                            act.wait_ge(pe_done["AT"], it.seen("AT", 1))
                            atleast(act, pe_done["WO"], it.seen("WO"))
                            nc.scalar.copy(actsT[:, :], src).then_inc(aT_copied, 1)
                        elif name == "WO":
                            act.wait_ge(pe_done["WO"], it.seen("WO", 1))
                            atleast(act, s_out, it.seen("WO"), 16)
                            nc.scalar.copy(s_sb[:, :], src).then_inc(s_copied, 1)
                        elif name == "xT":
                            act.wait_ge(pe_done["xT"], it.seen("xT", a + 1))
                            atleast(act, pe_done["H"], it.seen("H", max(a - 1, 0)))
                            nc.scalar.copy(xsT[:, a % 2, :], src[:, 0:P]).then_inc(xsT_copied, 1)
                        elif name == "tanh":
                            act.wait_ge(halves_read, it.seen("H", a + 1) * 2)
                            atleast(act, prod_done, it.seen("glu", max(a - 1, 0)))
                            nc.scalar.activation(tanh_g[:, a % 2, :], glu[:, a % 2, :], ACT.Tanh, scale=ALPHA / 2).then_inc(tanh_done, 1)
                        elif name == "hT":
                            act.wait_ge(pe_done["hT"], it.seen("hT", a + 1))
                            atleast(act, pe_done["y"], it.seen("y", max(a - 1, 0)))
                            nc.scalar.copy(hidT[:, a % 2, :, :].rearrange("p c n -> p (c n)"), src[:, 0:2 * P]).then_inc(hidT_copied, 1)
                        elif name == "y":
                            s = a % SLOTS
                            act.wait_ge(pe_done["y"], it.seen("y", a + 1))
                            atleast(act, y_out[s], it.seen(f"tile{s}", a // SLOTS), 16)
                            nc.scalar.copy(ys[:, s, :], src[:, 0:D]).then_inc(y_copied, 1)
                        elif name == "mix":
                            act.wait_ge(mix_step, MIX * a + 4)
                            nc.scalar.activation(y_in[a % 2][1], y_in[a % 2][0], ACT.Tanh, scale=0.5).then_inc(mix_tanh, 1)
            run_iterations(act, body)

        @block.vector
        def _(dve):
            n_r = [0]

            def link(ins):
                n_r[0] += 1
                ins.then_inc(r_dve, 1)
                dve.wait_ge(r_dve, n_r[0])

            v = nc.vector
            dve.wait_ge(weights_in, 16 * W_LOADS)
            link(v.tensor_scalar(braw[:, 32:40], braw[:, 32:40], 2.0, None, ALU.mult))
            link(v.tensor_copy(bparts[:, 0, :], braw[:, :]))
            link(v.tensor_tensor(braw[:, :], braw[:, :], bparts[:, 0, :], ALU.subtract))
            link(v.tensor_copy(bparts[:, 1, :], braw[:, :]))
            link(v.tensor_tensor(bparts[:, 2, :], braw[:, :], bparts[:, 1, :], ALU.subtract))
            link(v.tensor_scalar(gate[:, :], gate[:, :], scale[:, 0:1], None, ALU.mult))
            link(v.tensor_scalar(w1[:, :], w1[:, :], scale[:, 0:1], None, ALU.mult))
            v.memset(bank[:, PV_BANK, :], 0.0).then_inc(pv_zeroed, 1)
            for t in range(NT):
                if t % NQ == 0:
                    dve.wait_ge(x_in[t // NQ], 16)
                ins = v.bn_stats(stats[:, t, :], xall[:, t, :])
            link(ins)
            for t in range(NT):
                ins = v.bn_aggr(mv[:, t, :], stats[:, t, :])
            link(ins)
            link(v.tensor_scalar(va[:, :], mv[:, :, 1], EPS, None, ALU.add))
            assert n_r[0] == R_VAR

            def rsqrt(dst, n_act):
                dve.wait_ge(r_act, n_act)
                link(v.reciprocal(dst, sq[:, :]))
                link(v.tensor_tensor(rt[:, :], dst, dst, ALU.mult))
                link(v.tensor_tensor(rt[:, :], rt[:, :], va[:, :], ALU.mult))
                link(v.tensor_scalar(rt[:, :], rt[:, :], -0.5, 1.5, ALU.mult, ALU.add))
                link(v.tensor_tensor(dst, dst, rt[:, :], ALU.mult))
            rsqrt(rs[:, :], 1)
            for t in range(NT):
                v.tensor_scalar(xall[:, t, :], xall[:, t, :], mv[:, t, 0:1], rs[:, t:t + 1],
                                ALU.subtract, ALU.mult).then_inc(rows_ready, 1)
            link(v.tensor_tensor(rt[:, :], rs[:, :], rs[:, :], ALU.mult))
            link(v.tensor_tensor(rt[:, :], rt[:, :], mv[:, :, 1], ALU.mult))
            link(v.tensor_scalar(va[:, :], rt[:, :], EPS, None, ALU.add))
            assert n_r[0] == R_MS
            rsqrt(rr[:, :], 2)
            assert n_r[0] == R_RR
            def te(ap):
                return ap.rearrange("p (t e) -> p t e", e=E)

            def over_e(ap):
                return ap.unsqueeze(2).to_broadcast([P, NT, E])

            def over_t(ap):
                return ap.unsqueeze(1).to_broadcast([P, NT, E])
            dve.wait_ge(r_pe, B + 1)
            dve.wait_ge(consts_made, CONSTS)
            link(v.tensor_tensor(te(lg), te(bank[:, 6, 0:NE]), over_e(rr[:, :]), ALU.mult))
            link(v.tensor_tensor(te(lg), te(lg), over_t(gate_b[:, :]), ALU.add))

            def top(vm, oh):
                link(v.tensor_reduce(vm, te(lg), AX.X, ALU.max))
                link(v.tensor_tensor(te(sc1), te(lg), over_e(vm), ALU.is_ge))
                link(v.tensor_tensor(te(sc1), te(sc1), over_t(desc), ALU.mult))
                link(v.tensor_reduce(idf, te(sc1), AX.X, ALU.max))
                link(v.tensor_tensor(te(oh), over_t(desc), over_e(idf), ALU.is_equal))
            top(v1, oh1)
            link(v.scalar_tensor_tensor(te(lg), te(oh1), MASKED, te(lg), ALU.mult, ALU.add))
            top(v2, oh2)
            link(v.tensor_tensor(e2, v2, v1, ALU.subtract))
            assert n_r[0] == R_TOP
            link(v.tensor_tensor(cbf, oh1, oh2, ALU.add))
            assert n_r[0] == R_CNT
            dve.wait_ge(r_pe, B + 2)

            def et(ap):
                return ap.rearrange("p (e t) -> p e t", e=E)
            link(v.tensor_copy(et(tot), bank[:, 5, NE:2 * NE].rearrange("p (t e) -> p e t", e=E)))
            for e in range(E):
                ins = v.tensor_tensor_scan(et(inc)[:, e, :], onef, et(tot)[:, e, :], 0.0, ALU.mult, ALU.add)
            link(ins)
            link(v.tensor_tensor(et(cmpj), et(inc)[:, :, NT - 1:NT].to_broadcast([P, E, NT]),
                                 jot.unsqueeze(1).to_broadcast([P, E, NT]), ALU.is_gt))
            link(v.tensor_reduce(nte[:, 0:E], et(cmpj), AX.X, ALU.add))
            link(v.tensor_tensor_scan(cn[:, 0:E], onef[:, 0:E], nte[:, 0:E], 0.0, ALU.mult, ALU.add))
            link(v.tensor_tensor(start8, cn[:, 0:E], nte[:, 0:E], ALU.subtract))
            link(v.tensor_tensor(et(inc), et(inc), et(tot), ALU.subtract))
            link(v.tensor_tensor(te(posb), te(bank[:, 5, 0:NE]), et(inc).rearrange("p e t -> p t e"), ALU.add))
            link(v.scalar_tensor_tensor(te(posb), over_t(start8), float(P), te(posb), ALU.mult, ALU.add))
            for s, oh in enumerate((oh1, oh2)):
                link(v.tensor_tensor(sc2, oh, posb, ALU.mult))
                link(v.tensor_reduce(idf, te(sc2), AX.X, ALU.add))
                link(v.tensor_copy(index[:, s, :], idf))
            e_cmp = ecmp[0:1, :].rearrange("p (t e) -> p t e", e=E)
            link(v.tensor_tensor(e_cmp, tio[0:1, :].unsqueeze(2).to_broadcast([1, NF, E]),
                                 cn[0:1, 0:E].unsqueeze(1).to_broadcast([1, NF, E]), ALU.is_ge))
            link(v.tensor_reduce(esum[0:1, :], e_cmp, AX.X, ALU.add))
            link(v.tensor_scalar(expert[:, :], esum[0:1, :], float(E - 1), None, ALU.min))
            dve.wait_ge(r_act, R_ACT_T + B + 2)
            link(v.tensor_scalar(p1, e2, 1.0, None, ALU.add))
            link(v.reciprocal(p1, p1))
            link(v.tensor_scalar(wts[:, 0, :], p1, 0.5, None, ALU.mult))
            link(v.tensor_tensor(wts[:, 1, :], wts[:, 0, :], e2, ALU.mult))
            v.tensor_copy(rt[:, 0:1], p1[:, 0:1]).then_inc(routed, 1)

            def body(it):
                for k in range(STEPS):
                    if it.score:
                        u, j = k % UNITS, k // UNITS
                        hd = 2 * j + u // 2
                        dve.wait_ge(s_ready, it.seen("s", k + 1))
                        src = bank[:, S_BANK[k % 2], :]
                        if u == 4:
                            ins = v.tensor_reduce(rowmax[:, 1, 2 * j:2 * j + 2], src.rearrange("p (h k) -> p h k", h=2), AX.X, ALU.max)
                        elif u % 2 == 0:
                            ins = v.tensor_reduce(rowmax[:, 3, hd:hd + 1], src, AX.X, ALU.max)
                        else:
                            v.tensor_reduce(rowmax[:, 2, hd:hd + 1], src[:, 0:384], AX.X, ALU.max)
                            ins = v.tensor_reduce(rowmax[:, 0, hd:hd + 1], src[:, 384:512], AX.X, ALU.max)
                        ins.then_inc(max_done, 1)
                    for name, a in it.plan[k]:
                        if name in RING:
                            r = ring_of(it, name, a)
                            src = bank[:, RING_BANK[r % 3], :]
                        if name == "msplit":
                            done = it.seen("msplit", 0 if a or not it.attend else 1)
                            dve.wait_ge(max_done, it.seen("s", 0 if a else 20))
                            atleast(dve, pe_done["mT"], done)
                            mx = rowmax[:, :, a * HALF:(a + 1) * HALF]
                            nm = msplit[:, a, :, :, :]

                            def then(ins, n):
                                ins.then_inc(split_done, 1)
                                dve.wait_ge(split_done, done * 4 + n)
                            then(v.tensor_scalar(nm[:, :, 0, :], mx, -1.0, None, ALU.mult), 1)
                            then(v.scalar_tensor_tensor(mrest[:, :, :], mx, -1.0, nm[:, :, 0, :], ALU.mult, ALU.subtract), 2)
                            then(v.tensor_copy(nm[:, :, 1, :], mrest[:, :, :]), 3)
                            v.tensor_tensor(nm[:, :, 2, :], mrest[:, :, :], nm[:, :, 1, :], ALU.subtract).then_inc(split_done, 1)
                        elif name == "Q":
                            dve.wait_ge(pe_done["Q"], it.seen("Q", a + 1))
                            if a == 0:
                                atleast(dve, low_done, it.seen("low"))
                            dst, tab = ((qk, cos), (qk_sin, sin))[a % 2]
                            v.tensor_tensor(dst[:, a // 2, :], src, tab[:, :], ALU.mult).then_inc(roped, 1)
                        elif name == "H":
                            dve.wait_ge(pe_done["H"], it.seen("H", a + 1))
                            v.tensor_scalar(glu[:, a % 2, :], src[:, 0:I], LIMIT, None, ALU.min).then_inc(halves_read, 1)
                            atleast(dve, pe_done["hT"], it.seen("hT", max(a - 1, 0)))
                            v.tensor_scalar(lin[:, a % 2, :], src[:, I:2 * I], LIMIT, -LIMIT, ALU.min, ALU.max).then_inc(halves_read, 1)
                        elif name == "glu":
                            dve.wait_ge(tanh_done, it.seen("tanh", a + 1))
                            v.scalar_tensor_tensor(glu[:, a % 2, :], tanh_g[:, a % 2, :], 1.0, glu[:, a % 2, :],
                                                   ALU.add, ALU.mult).then_inc(prod_done, 1)
                            dve.wait_ge(prod_done, it.seen("glu", a + 1))
                            v.scalar_tensor_tensor(hid[:, a % 2, :], lin[:, a % 2, :], 1.0, glu[:, a % 2, :],
                                                   ALU.add, ALU.mult).then_inc(hid_done, 1)
                        elif name == "OT":
                            n = it.seen("OT", (a + 1) % 4 if it.i >= 1 else a)
                            dve.wait_ge(pe_done["OT"], n + 1)
                            o4 = src.rearrange("p (t c r) -> p t c r", t=NQ, c=HG)
                            v.reciprocal(recip[:, :, :], o4[:, :, :, DH]).then_inc(recip_done, 1)
                            dve.wait_ge(recip_done, n + 1)
                            atleast(dve, s_out, it.seen("WO", 0 if a == 3 or it.i < 1 else 1), 16)
                            dst = acts[:, :].rearrange("p (t g c d) -> p t g c d", t=NQ, g=NG, c=HG)[:, :, a, :, :]
                            v.tensor_tensor(dst, o4[:, :, :, 0:DH], recip[:, :, :].unsqueeze(3).to_broadcast([P, NQ, HG, DH]),
                                            ALU.mult).then_inc(acts_done, 1)
                        elif name == "mix":
                            y1, y2 = y_in[a % 2]
                            wt = [wts[:, s, NQ * a:NQ * (a + 1)].unsqueeze(2).to_broadcast([P, NQ, D]) for s in range(2)]

                            def then(ins, n):
                                ins.then_inc(mix_step, 1)
                                dve.wait_ge(mix_step, MIX * a + n)
                            dve.wait_ge(gathered[a % 2], 16 * 8 * (a // 2 + 1))
                            v.tensor_tensor(y1, y1, wt[0], ALU.mult).then_inc(mix_step, 1)
                            then(v.tensor_tensor(y2, y2, wt[1], ALU.mult), 2)
                            then(v.tensor_tensor(y1, y1, y2, ALU.add), 3)
                            dve.wait_ge(c_in, 48 * (a + 1))
                            then(v.tensor_tensor(y1, y1, xn_c, ALU.add), 4)
                            dve.wait_ge(mix_tanh, a + 1)
                            then(v.scalar_tensor_tensor(y1, y2, 1.0, y1, ALU.add, ALU.mult), 5)
                            then(v.tensor_tensor(y1, y1, s_c, ALU.mult), 6)
                            atleast(dve, out_done, a, 16)
                            then(v.scalar_tensor_tensor(t_c, y1, 0.5, x_c, ALU.mult, ALU.add), 7)
            run_iterations(dve, body)

        @block.tensor
        def _(pe):
            pe.wait_ge(consts_made, CONSTS)
            pe.wait_ge(pv_zeroed, 1)
            for b in range(B):
                pe.wait_ge(rows_ready, NQ * (b + 1))
                if b >= 4:
                    pe.wait_ge(r_act, R_ACT_T + b - 3)
                for t in range(NQ):
                    ins = nc.tensor.transpose(bank[:, b % 4, P * t:P * (t + 1)], xall[:, NQ * b + t, :], ident[:, :])
                ins.then_inc(r_pe, 1)
            xnT = probs[:, 0, :, :].rearrange("p a b -> p (a b)")
            pe.wait_ge(r_act, R_ACT_T + B)
            for t in range(NT):
                ins = nc.tensor.matmul(bank[:, 6, E * t:E * (t + 1)], xnT[:, P * t:P * (t + 1)], gate[:, :], start=True, stop=True)
            ins.then_inc(r_pe, 1)
            pe.wait_ge(r_dve, R_CNT)
            nc.tensor.matmul(bank[:, 5, 0:NE], ltri[:, :], cbf, start=True, stop=True)
            nc.tensor.matmul(bank[:, 5, NE:2 * NE], onesb[:, :], cbf, start=True, stop=True).then_inc(r_pe, 1)
            pe.wait_ge(routed, 1)

            def score_keys_by_queries(it, k):
                u, j, par = k % UNITS, k // UNITS, it.i % 2
                ha, hb = 2 * j, 2 * j + 1
                if k in (0, STEPS // 2):
                    pe.wait_ge(m_in[k // 20], it.seen("mT0") * 16 if k == 0 else it.seen("mT1", 1) * 16)
                atleast(pe, exp_done, it.seen("st", k - 1))
                out = bank[:, ST_BANK[k % 2], :]
                todo = {0: ((ha, 0, 0),), 1: ((ha, 3, 0), (ha, 1, 128)), 2: ((hb, 0, 0),), 3: ((hb, 3, 0), (hb, 1, 128)),
                        4: ((ha, 2, 0), (hb, 2, 256))}[u]
                for h, kt, col in todo:
                    n = S - P * kt
                    ins = nc.tensor.matmul(out[:, col:col + n], ks[par][:, h, P * kt:P * (kt + 1)],
                                           qs[par][:, h, P * kt:S], start=True, stop=True)
                ins.then_inc(st_ready, 1)

            def score_queries_by_keys(it, k):
                u, j, par = k % UNITS, k // UNITS, (it.i + 1) % 2
                ha, hb = 2 * j, 2 * j + 1
                if k in (0, STEPS // 2):
                    pe.wait_ge(stack_in[k // 20], it.seen(f"stack{k // 20}") * (16 * 9))
                atleast(pe, max_done, it.seen("s", k - 1))
                out = bank[:, S_BANK[k % 2], :]
                todo = {0: ((ha, 3, 0),), 1: ((ha, 2, 0), (ha, 0, 384)), 2: ((hb, 3, 0),), 3: ((hb, 2, 0), (hb, 0, 384)),
                        4: ((ha, 1, 0), (hb, 1, 256))}[u]
                for n, (h, qt, col) in enumerate(todo):
                    w = P * (qt + 1)
                    nc.tensor.matmul(out[:, col:col + w], qs[par][0:MROW, h, P * qt:P * (qt + 1)],
                                     ks[par][0:MROW, h, 0:w], start=(n == 0), stop=False, skip_group_check=True)
                if u == 4:
                    dst, m = out.rearrange("p (h k q) -> p h k q", h=2, k=2)[:, :, 1, :], mask2[:, :, :]
                elif u % 2:
                    dst, m = out[:, 256:512].rearrange("p (k q) -> p k q", k=2), mask2[:, :, :]
                else:
                    dst, m = out[:, 384:512], mask2[:, 0, :]
                nc.tensor.matmul(dst, identb[:, :], m, start=False, stop=True, skip_group_check=True).then_inc(s_ready, 1)

            def body(it):
                ring = it.ring()
                r = 0
                for k in range(STEPS):
                    if it.attend:
                        score_keys_by_queries(it, k)
                    if it.score:
                        score_queries_by_keys(it, k)
                    for name, a in it.plan[k]:
                        if name == "pv":
                            n = it.seen("pv", (a + 1) % 4 if it.i >= 1 else a)
                            pe.wait_ge(selected, (n + 1) * (2 * SELECTS))
                            atleast(pe, o_copied, n)
                            if a == 0:
                                pe.wait_ge(v_copied, it.seen("V", 1))
                            for kt in range(NQ):
                                for c in range(HG):
                                    w = S - P * kt
                                    ins = nc.tensor.matmul(bank[32 * c:32 * c + VC, PV_BANK, P * kt:S], vs[:, kt, HG * a + c, :],
                                                           probs[:, a % 2, c, PT_AT[kt]:PT_AT[kt] + w],
                                                           start=(kt == 0), stop=(kt == NQ - 1), skip_group_check=True)
                            ins.then_inc(pv_done, 1)
                        if name not in RING:
                            continue
                        if r == 0:
                            for nm, (sm, each) in reader.items():
                                atleast(pe, sm, it.seen(nm), each)
                        elif r >= 3:
                            nm, _, j = ring[r - 3]
                            sm, each = reader[nm]
                            atleast(pe, sm, it.seen(nm, j + 1), each)
                        dst = bank[:, RING_BANK[r % 3], :]
                        r += 1
                        if name == "Q":
                            if a == 0:
                                atleast(pe, xq_in, it.seen("sum", 1), 16)
                            ins = nc.tensor.matmul(dst, wq[:, P * a:P * (a + 1)], xp[:, :], start=True, stop=True)
                        elif name == "V":
                            atleast(pe, xv_in, it.seen("V", 1), 16)
                            for t in range(NQ):
                                ins = nc.tensor.matmul(dst[:, P * t:P * (t + 1)], xp[:, P * t:P * (t + 1)], wv[:, :], start=True, stop=True)
                        elif name == "mT":
                            pe.wait_ge(split_done, (mt_seen(it, a) + 1) * 4)
                            for t in range(NQ):
                                ins = nc.tensor.transpose(dst.bitcast(BF16)[0:3 * HALF, P * t:P * (t + 1)],
                                                          msplit[:, a, t, :, :].rearrange("p c h -> p (c h)"), identb[:, :])
                        elif name == "OT":
                            n = it.seen("OT", (a + 1) % 4 if it.i >= 1 else a)
                            pe.wait_ge(o_copied, n + 1)
                            for t in range(NQ):
                                ins = nc.tensor.transpose(dst[:, P * t:P * (t + 1)], o_sb[:, P * t:P * (t + 1)], ident[:, :])
                        elif name == "AT":
                            pe.wait_ge(acts_done, it.seen("OT", 1))
                            for t in range(NQ):
                                ins = nc.tensor.transpose(dst[:, P * t:P * (t + 1)], acts[:, P * t:P * (t + 1)], ident[:, :])
                        elif name == "WO":
                            pe.wait_ge(aT_copied, it.seen("AT", 1))
                            for t in range(NQ):
                                ins = nc.tensor.matmul(dst[:, P * t:P * (t + 1)], actsT[:, P * t:P * (t + 1)], wo[:, :], start=True, stop=True)
                        elif name == "xT":
                            pe.wait_ge(xs_in[a % SLOTS], it.seen(f"tile{a % SLOTS}", a // SLOTS + 1) * 16)
                            ins = nc.tensor.transpose(dst[:, 0:P], xs[:, a % SLOTS, :], ident[:, :])
                        elif name == "H":
                            pe.wait_ge(xsT_copied, it.seen("xT", a + 1))
                            if it.i == 1:
                                pe.wait_ge(bias_in, 16)
                            e = pe.value_load(expert[0:1, bass.ds(it.tile(a), 1)], min_val=0, max_val=E - 1)
                            nc.tensor.matmul(dst, xsT[:, a % 2, :], w1[:, bass.ds(e * (2 * I), 2 * I)], start=True, stop=False)
                            ins = nc.tensor.matmul(dst, ones3[:, :], bias[:, bass.ds(e * (2 * I), 2 * I)], start=False, stop=True)
                        elif name == "hT":
                            pe.wait_ge(hid_done, it.seen("glu", a + 1))
                            for c in range(2):
                                ins = nc.tensor.transpose(dst[:, P * c:P * (c + 1)], hid[:, a % 2, P * c:P * (c + 1)], ident[:, :])
                        elif name == "y":
                            pe.wait_ge(hidT_copied, it.seen("hT", a + 1))
                            e = pe.value_load(expert[0:1, bass.ds(it.tile(a), 1)], min_val=0, max_val=E - 1)
                            for c in range(2):
                                nc.tensor.matmul(dst[:, 0:D], hidT[:, a % 2, c, :], w2[:, bass.ds(e * (2 * D) + c * D, D)],
                                                 start=(c == 0), stop=False)
                            ins = nc.tensor.matmul(dst[:, 0:D], ones3[:, :], bias[:, bass.ds(e * D + E * 2 * I, D)], start=False, stop=True)
                        ins.then_inc(pe_done[name], 1)
            run_iterations(pe, body)


CONSTS = 21
R_VAR, R_MS, R_RR, R_TOP, R_CNT, R_ACT_T = 10, 18, 23, 37, 38, 2


def rope_tables():
    inv = (1.0 / np.float32(THETA) ** (np.arange(0, DH, 2, dtype=np.float32) / np.float32(DH))).astype(np.float32)
    f = np.arange(S, dtype=np.float32)[None, :] * inv[:, None]
    cos, sin = np.cos(f.astype(np.float64)), np.sin(f.astype(np.float64))
    cos = np.repeat(cos, 2, axis=0)
    sin = np.stack([-sin, sin], axis=1).reshape(DH, S)
    return tuple(np.ascontiguousarray(np.repeat(t, H, axis=0).astype(np.float32)) for t in (cos, sin))


def kernel(L0_attn_X, L0_attn_W_KQV, L0_attn_W_O, L0_ffn_norm_scale, L0_ffn_gate_w, L0_ffn_gate_b,
           L0_ffn_mlp1_w, L0_ffn_mlp1_b, L0_ffn_mlp2_w, L0_ffn_mlp2_b):
    import concourse.bacc as _bacc
    from concourse.bass_utils import run_bass_kernel_spmd as _run

    c = np.ascontiguousarray
    wt = np.asarray(L0_attn_W_KQV)
    order = np.array([h * DH + d for d in range(DH) for h in range(H)])
    swapped = np.array([h * DH + (d ^ 1) for d in range(DH) for h in range(H)])
    wk, wqm, wvm = wt[0:D], wt[D:2 * D], wt[2 * D:3 * D]
    wq = np.concatenate([wqm[order], wqm[swapped], wk[order], wk[swapped]], axis=0).T
    w1 = np.asarray(L0_ffn_mlp1_w).reshape(E, D, I, 2).transpose(1, 0, 3, 2).reshape(D, E * 2 * I)
    b1 = np.asarray(L0_ffn_mlp1_b).reshape(E, I, 2).transpose(0, 2, 1).reshape(P, E * 2 * I // P)
    w2 = np.asarray(L0_ffn_mlp2_w).reshape(E, 2, P, D).transpose(2, 0, 1, 3).reshape(P, E * 2 * D)
    cos, sin = rope_tables()
    arrays = {
        "x": np.asarray(L0_attn_X).reshape(B * S, D), "wq": wq, "wv": wvm.T, "wo": np.asarray(L0_attn_W_O).T,
        "cos_t": cos, "sin_t": sin, "norm_scale": np.asarray(L0_ffn_norm_scale).reshape(D, 1),
        "gate_w": np.asarray(L0_ffn_gate_w), "gate_bias": np.asarray(L0_ffn_gate_b).reshape(1, E),
        "w1_t": w1, "b1_t": b1, "w2_t": w2, "b2_t": np.asarray(L0_ffn_mlp2_b).reshape(P, E * D // P),
    }
    arrays = {n: c(a) for n, a in arrays.items()}
    nc = _bacc.Bacc("TRN2", target_bir_lowering=False, num_devices=1)
    aps = [nc.dram_tensor("in_" + n, a.shape, mybir.dt.from_np(a.dtype), kind="ExternalInput").ap() for n, a in arrays.items()]
    out = nc.dram_tensor("out", (B * S, D), F32, kind="ExternalOutput").ap()
    nc.disable_value_cache = True
    build(nc, *aps, out)
    r = _run(nc, [{"in_" + n: a for n, a in arrays.items()}], core_ids=[0])
    return r.results[0]["out"].reshape(B, S, D)
```

```python
from contextlib import ExitStack

import numpy as np

import concourse.bass as bass
from concourse import mybir

F32 = mybir.dt.float32
BF16 = mybir.dt.bfloat16
I32 = mybir.dt.int32
U32 = mybir.dt.uint32
ALU = mybir.AluOpType
ACT = mybir.ActivationFunctionType
AX = mybir.AxisListType

P = 128
B, S, D = 8, 512, 128
H, DH = 16, 8
E, I = 8, 256
NQ = S // P
NT = B * NQ
HG = 4
NG = H // HG
HALF = H // 2
VC = 16
LIMIT, ALPHA, EPS, THETA = 7.0, 1.702, 1e-5, 10000.0
MASKED = -1e30

K_PART = (0, 0, 0, 1, 1, 2)
Q_PART = (0, 1, 2, 0, 1, 0)
MROW = 96

PT_AT = (0, 640, 1024, 512)
PT_COLS = 1280
UNITS = 5
STEPS = UNITS * H // 2

NF = (B * S * 2) // P + E
XBUF, FBUF = 3, 3
SELECTS = 3


def every_512(head):
    return bass.AP(tensor=head.tensor, offset=head.offset, ap=[head.ap[0], [512, 3], [1, P]])


def timeline():
    at = {i: [[] for _ in range(STEPS)] for i in range(-2, B + 2)}

    def put(i, k, name, which):
        at[i + k // STEPS][k % STEPS].append((name, which))

    for b in range(B):
        i = b - 2
        q0 = 11 if i >= 0 else 1
        if b >= 2:
            put(i, q0 - 3, "xq", b)
        for c in range(4):
            put(i, q0 + c, "Q", (b, c))
        for name, k in (("sum", 4), ("hi", 5), ("rest", 7), ("mid", 8), ("low", 10), ("parts", 11)):
            put(i, q0 + k, name, b)
        put(i, 25 if i >= 0 else q0 + 12, "stack", (b, 0))
        put(i, 39 if i >= 0 else q0 + 13, "stack", (b, 1))
        for f in range(2):
            k = 20 * (f + 1)
            put(b - 1, k, "msplit", (b, f))
            put(b - 1, k + 2, "mT", (b, f))
            put(b - 1, k + 2, "mout", (b, f))
            put(b - 1, k + 4, "min", (b, f))
        put(b, 5, "xv", b)
        put(b, 7, "V", b)
        for j in range(H // 2):
            put(b, 5 * j + 5, "sel", (b, j))
        for g in range(NG):
            for kt in range(NQ):
                put(b, 10 * g + 12 + kt, "pv", (b, g, kt))
            put(b, 10 * g + 16, "oc", (b, g))
            put(b, 10 * g + 18, "OT", (b, g))
        put(b, 50, "AT", b)
        put(b, 52, "WO", b)
    put(-2, 5, "logits", 0)
    put(-2, 6, "rank", 0)
    put(-2, 6, "route", 0)
    put(-2, 8, "wload", 0)
    put(-2, 13, "rowt", 0)
    put(-2, 14, "e2", 0)
    put(-2, 15, "weigh", 0)
    put(-2, 20, "bias", 0)
    put(-1, 30, "bload", 0)
    for n in range(2 * NT):
        put(-1 if n < SCATTER_FIRST else 0, n if n < SCATTER_FIRST else (n - SCATTER_FIRST), "scatter", n)
    for n in range(NF + 3):
        i, k = 1 + n // SLOTS, (n % SLOTS) * STEPS // SLOTS
        if n < NF:
            put(i, k - 3 if n >= 2 else 0, "xload", n)
            put(i, k + 2, "H", n)
            put(i, k + 3, "tanh", n)
            put(i, k + 4, "glu", n)
        put(i, k, "F", n)
        if n >= 3:
            put(i, k + 1, "yout", n)
    for c in range(B):
        i, k = (6, 10 * c) if c < 4 else (7, 9 * (c - 4))
        for r in range(2 * NQ):
            put(i, k + r, "gather", (c, r))
        put(i, k + 8, "cload", c)
        for m, d in enumerate((9, 10, 11, 12, 14)):
            put(i, k + d, "mix", (c, m))
        put(i, k + 13, "mtanh", c)
        late = (8 - i) * STEPS + 13 if c == B - 1 else k + 8
        put(i, late, "sload", c)
        late = late + 1 if c == B - 1 else k + 15
        put(i, late, "mix", (c, 5))
        put(i, late + 1, "mix", (c, 6))
        put(i, late + 2, "out", c)
    return at


SLOTS = 15
SCATTER_FIRST = 28
TIMELINE = timeline()
RING = ("Q", "V", "F", "H", "OT", "mT", "AT", "WO")
MIX = 7


def ordinals():
    nth, count, ring = {}, {}, []
    for i, steps in TIMELINE.items():
        for step in steps:
            for name, which in step:
                count[name] = count.get(name, 0) + 1
                nth[name, which] = count[name]
                if name in RING:
                    ring.append((name, which))
    return nth, ring


NTH, RING_USERS = ordinals()
RING_AT = {user: n for n, user in enumerate(RING_USERS)}


def steps():
    for i, ks in TIMELINE.items():
        for k, events in enumerate(ks):
            yield i, k, events


def atleast(eng, sem, n):
    if n > 0:
        eng.wait_ge(sem, n)



def build(nc, x_h, wq_h, wv_h, wo_h, cos_h, sin_h, scale_h, gate_w_h, gate_b_h, w1_h, b1_h, w2_h, b2_h, out_h):
    ctx = ExitStack()
    with ctx:
        def sb(name, shape, dt=F32):
            return ctx.enter_context(nc.sbuf_tensor(name, shape, dt))

        def sem(name):
            return ctx.enter_context(nc.semaphore(name))

        w1 = sb("w1", [P, E * 2 * I])
        w2 = sb("w2", [P, E * 2 * D])
        bias = sb("bias", [3, E * 2 * I + E * D], BF16)
        wq, wv, wo = sb("wq", [P, 4 * P]), sb("wv", [P, D]), sb("wo", [P, D])
        cos, sin = sb("cos", [P, S]), sb("sin", [P, S])
        xall = sb("xall", [P, NT, D])
        qs = [sb(f"qs{n}", [P, H, S], BF16) for n in range(2)]
        ks = [sb(f"ks{n}", [P, H, S], BF16) for n in range(2)]
        probs = sb("probs", [P, 2, HG, PT_COLS])
        vs = sb("vs", [P, NQ, H, VC])
        o_sb, acts, actsT = (sb(n, [P, S]) for n in ("o_sb", "acts", "actsT"))
        s_sb = acts
        qk = sb("qk", [P, 2, S])
        qk_sin = sb("qk_sin", [P, 2, S])
        parts = sb("parts", [P, 2, 3, S], BF16)
        xp = sb("xp", [P, S])
        xs = sb("xs", [P, XBUF, D])
        slot = sb("slot", [P, FBUF, S])
        glu, lin, tanh_g = (sb(n, [P, 2, I]) for n in ("glu", "lin", "tanh_g"))
        hid = lin
        rowmax = sb("rowmax", [P, NQ, H])
        msplit = sb("msplit", [P, 2, NQ, 3, HALF], BF16)
        mrest = sb("mrest", [P, NQ, HALF])
        mT = sb("mT", [3 * HALF, 2, S], BF16)
        recip = sb("recip", [P, NQ, HG])
        ident, identb = sb("ident", [P, P]), sb("identb", [P, P], BF16)
        mask2 = sb("mask2", [P, 2, P], BF16)
        ones3 = sb("ones3", [3, P], BF16)
        ltri, onesb = sb("ltri", [P, P], BF16), sb("onesb", [P, P], BF16)
        scale, gate = sb("scale", [P, 1]), sb("gate", [P, E])
        gate_b = sb("gate_b", [P, E])
        stats, mv = o_sb[:, 256:256 + NT * 6].rearrange("p (t s) -> p t s", s=6), sb("mv", [P, NT, 2])
        rs, rr, rt = sb("rs", [P, NT]), sb("rr", [P, NT]), sb("rt", [P, NT])
        sq, va = sb("sq", [P, NT]), sb("va", [P, NT])
        bparts = sb("bparts", [P, 3, 40], BF16)
        braw = sb("braw", [P, 40])
        wts = sb("wts", [P, 2, NT])
        index = sb("index", [P, 2, NT], U32)
        expert = sb("expert", [1, NF], I32)

        bank = ctx.enter_context(nc.psum_tensor("bank", [P, 8, 512], F32))
        ST_BANK, S_BANK, PV_BANK, RING_BANK = (0, 1), (2, 3), 4, (5, 6, 7)
        LOGIT_BANK, RANK_BANK = S_BANK

        X_AT, HID_AT, Y_AT = slice(0, P), slice(P, 3 * P), slice(3 * P, 4 * P)

        NE = NT * E
        lg, oh1, oh2, sc1, sc2, posb = (t[:, n, :] for t in (glu, lin, tanh_g) for n in range(2))
        tot, inc, cmpj = (actsT[:, 0:NE], actsT[:, NE:2 * NE], acts[:, 0:NE])
        cbf = acts[:, NE:NE + NE // 2].bitcast(BF16)
        small = slot[:, 0, :]
        desc, jot, onef, v1, v2, nte, cn, e2, p1, idf = (small[:, NT * n:NT * (n + 1)] for n in range(10))
        desc = desc[:, 0:E]
        tio = small[:, NT * 10:NT * 10 + NF]
        ecmp = slot[:, 1:3, :].rearrange("p a b -> p (a b)")[:, 0:NF * E]
        esum, start8 = o_sb[:, 0:NF], o_sb[:, P:P + E]
        xnT = probs[:, 0, :, :].rearrange("p a b -> p (a b)")
        zero = probs[:, 1, 0:2, :].rearrange("p a b -> p (a b)")[:, 0:NF * D // 4]

        def cbuf(n):
            return xall[:, NQ * n:NQ * (n + 1), :]
        y_in = [[cbuf(0), cbuf(1)], [cbuf(2), cbuf(3)]]
        x_c, xn_c, s_c, t_c = cbuf(4), cbuf(5), cbuf(6), cbuf(7)

        def dram(name, shape, dt=F32):
            return nc.dram_tensor(name, shape, dt).ap()
        xnT_d = dram("xnT_d", (P, B * S))
        xn_d = dram("xn_d", (B * S, D))
        s_d = dram("s_d", (B * S, D))
        sorted_d = dram("sorted_d", (NF * P, D))
        y_d = dram("y_d", (NF * P, D))
        parts_d = dram("parts_d", (2, 2, 3, DH, H * S), BF16)
        m_d = dram("m_d", (2, 3, HALF * S), BF16)
        bias_d = dram("bias_d", (3, E * 2 * I + E * D), BF16)

        small_in, big_in = sem("small_in"), sem("big_in")
        ident_made, consts_made, stacks_made = sem("ident_made"), sem("consts_made"), sem("stacks_made")
        zeroed, zero_rows, xn_out, xnT_out, bias_out, bias_in = (sem(n) for n in (
            "zeroed", "zero_rows", "xn_out", "xnT_out", "bias_out", "bias_in"))
        scattered, routed, rows_scaled, weights_made = (sem(n) for n in (
            "scattered", "routed", "rows_scaled", "weights_made"))
        x_in = [sem(f"x_in{n}") for n in range(B)]
        r_dve, sq_done, xnT_copied, e2_done = sem("r_dve"), sem("sq_done"), sem("xnT_copied"), sem("e2_done")
        xnT_ready, logits_ready, ranks_ready = sem("xnT_ready"), sem("logits_ready"), sem("ranks_ready")
        rows_ready = sem("rows_ready")
        st_ready, exp_done, s_ready, max_done = (sem(n) for n in ("st_ready", "exp_done", "s_ready", "max_done"))
        selected, pv_done, o_copied, acts_done = (sem(n) for n in ("selected", "pv_done", "o_copied", "acts_done"))
        recip_done, pv_zeroed = sem("recip_done"), sem("pv_zeroed")
        split_done, m_written = sem("split_done"), [sem(f"m_written{n}") for n in range(2)]
        m_in = [sem(f"m_in{n}") for n in range(2)]
        stack_in = [[sem(f"stack{par}_in{half}") for half in range(2)] for par in range(2)]
        xq_in, xv_in = sem("xq_in"), sem("xv_in")
        roped, qk_sum, hi_done, rest_done, mid_done, low_done, parts_out = (sem(n) for n in (
            "roped", "qk_sum", "hi_done", "rest_done", "mid_done", "low_done", "parts_out"))
        ready = {n: sem(f"{n}_ready") for n in RING}
        mT_copied, v_copied, aT_copied, s_copied, s_out = (sem(n) for n in (
            "mT_copied", "v_copied", "aT_copied", "s_copied", "s_out"))
        xs_in = [sem(f"xs_in{n}") for n in range(XBUF)]
        y_out = [sem(f"y_out{n}") for n in range(FBUF)]
        slot_copied, halves_read, tanh_done, prod_done, hid_done = (sem(n) for n in (
            "slot_copied", "halves_read", "tanh_done", "prod_done", "hid_done"))
        c_in, s_in, mix_step, mix_tanh, out_done = (sem(n) for n in ("c_in", "s_in", "mix_step", "mix_tanh", "out_done"))
        gathered = [sem("gathered0"), sem("gathered1")]

        reader = {"Q": (roped, 1), "V": (v_copied, 1), "F": (slot_copied, 1), "H": (halves_read, 2),
                  "OT": (acts_done, 1), "mT": (mT_copied, 1), "AT": (aT_copied, 1), "WO": (s_copied, 1)}

        def ring_bank(user):
            return bank[:, RING_BANK[RING_AT[user] % 3], :]

        def st_units(b, k):
            return b * STEPS + k + 1

        block = ctx.enter_context(nc.Block())

        @block.sync
        def _(sp):
            x_rows = x_h.rearrange("(b t p) d -> b p t d", p=P, t=NQ)
            xn_rows = xn_d.rearrange("(b t p) d -> b p t d", p=P, t=NQ)
            s_rows = s_d.rearrange("(b t p) d -> b p t d", p=P, t=NQ)
            out_rows = out_h.rearrange("(b t p) d -> b p t d", p=P, t=NQ)
            for b in range(B):
                sp.dma_start(xall[:, NQ * b:NQ * (b + 1), :], x_rows[b]).then_inc(x_in[b], 16)
            for dst, src in ((wq[:, :], wq_h), (scale[:, :], scale_h), (gate[:, :], gate_w_h), (cos[:, :], cos_h),
                             (sin[:, :], sin_h),
                             (gate_b[:, :], gate_b_h.partition_broadcast(P).rearrange("p a e -> p (a e)")),
                             (wv[:, :], wv_h), (wo[:, :], wo_h), (braw[:, 0:32], b1_h), (braw[:, 32:40], b2_h)):
                sp.dma_start(dst, src).then_inc(small_in, 16)
            for b in range(B):
                sp.wait_ge(rows_ready, NQ * (b + 1))
                sp.dma_start(xn_rows[b], xall[:, NQ * b:NQ * (b + 1), :]).then_inc(xn_out, 16)
            for b in range(B):
                sp.wait_ge(xnT_copied, b + 1)
                sp.dma_start(xnT_d[:, b * S:(b + 1) * S], xnT[:, b * S:(b + 1) * S]).then_inc(xnT_out, 16)
            sp.wait_ge(zeroed, 1)
            z_d = sorted_d.rearrange("(p q r) d -> q p (r d)", p=P, q=4)
            for q in range(4):
                sp.dma_start(z_d[q], zero).then_inc(zero_rows, 16)

            for i, k, events in steps():
                for name, a in events:
                    if name == "xv":
                        if a == 0:
                            sp.wait_ge(xnT_out, 16 * B)
                        sp.wait_ge(ready["Q"], NTH["Q", (min(a + 1, B - 1), 3)])
                        sp.dma_start(xp[:, :], xnT_d[:, a * S:(a + 1) * S]).then_inc(xv_in, 16)
                    elif name == "xq":
                        sp.wait_ge(ready["V"], NTH["V", a - 2])
                        sp.dma_start(xp[:, :], xnT_d[:, a * S:(a + 1) * S]).then_inc(xq_in, 16)
                    elif name == "mout":
                        b, f = a
                        sp.wait_ge(mT_copied, NTH["mT", a])
                        atleast(sp, m_in[f], 16 * b)
                        sp.dma_start(m_d[f].rearrange("c (h q) -> (c h) q", h=HALF), mT[:, f, :]).then_inc(m_written[f], 16)
                    elif name == "min":
                        b, f = a
                        sp.wait_ge(m_written[f], 16 * (b + 1))
                        if b < 2:
                            sp.wait_ge(stacks_made, STACK_SETS)
                        sp.dma_start(qs[b % 2][MROW:MROW + 3, f * HALF:(f + 1) * HALF, :], m_d[f]).then_inc(m_in[f], 16)
                    elif name == "parts":
                        sp.wait_ge(low_done, NTH["low", a])
                        for half in range(2):
                            atleast(sp, stack_in[a % 2][half], STACK_LOADS * 16 * (a // 2))
                        sp.dma_start(parts_d[a % 2].rearrange("a c d (h q) -> (d h) (a c) q", h=H),
                                     parts[:, :, :, :].rearrange("p a c q -> p (a c) q")).then_inc(parts_out, 16)
                    elif name == "stack":
                        b, half = a
                        sp.wait_ge(parts_out, 16 * (b + 1))
                        if b < 2:
                            sp.wait_ge(stacks_made, STACK_SETS)
                        else:
                            sp.wait_ge(st_ready, st_units(b - 2, STEPS // 2 * (half + 1) - 1))
                        src, h0 = parts_d[b % 2], half * HALF
                        loads = [(qs, 0, 0, 0, 3), (qs, 24, 0, 0, 2), (qs, 40, 0, 0, 1)]
                        loads += [(ks, DH * r, 1, part, 1) for r, part in enumerate(K_PART)]
                        assert len(loads) == STACK_LOADS
                        for t, row, qk_at, lo, n in loads:
                            sp.dma_start(t[b % 2][row:row + DH * n, h0:h0 + HALF, :],
                                         src[qk_at, lo:lo + n, :, h0 * S:(h0 + HALF) * S].rearrange("c d x -> (c d) x")
                                         ).then_inc(stack_in[b % 2][half], 16)
                    elif name == "wload":
                        sp.dma_start(w1[:, :], w1_h).then_inc(big_in, 16)
                        sp.dma_start(w2[:, :], w2_h).then_inc(big_in, 16)
                    elif name == "bload":
                        sp.wait_ge(weights_made, 1)
                        n1 = E * 2 * I
                        sp.dma_start(bias_d[:, 0:n1].rearrange("c (p j) -> p c j", p=P), bparts[:, :, 0:32]).then_inc(bias_out, 16)
                        sp.dma_start(bias_d[:, n1:].rearrange("c (p j) -> p c j", p=P), bparts[:, :, 32:40]).then_inc(bias_out, 16)
                        sp.wait_ge(bias_out, 32)
                        sp.dma_start(bias[:, :], bias_d).then_inc(bias_in, 16)
                    elif name == "xload":
                        if a == 0:
                            sp.wait_ge(scattered, 16 * 2 * NT)
                        atleast(sp, ready["F"], a - XBUF + 1)
                        sp.dma_start(xs[:, a % XBUF, :], sorted_d[a * P:(a + 1) * P, :]).then_inc(xs_in[a % XBUF], 16)
                    elif name == "yout":
                        sp.wait_ge(slot_copied, a + 1)
                        sp.dma_start(y_d[(a - 3) * P:(a - 2) * P, :], slot[:, a % FBUF, Y_AT]).then_inc(y_out[a % FBUF], 16)
                    elif name == "WO":
                        sp.wait_ge(s_copied, a + 1)
                        sp.dma_start(s_rows[a], s_sb[:, :].rearrange("p (t d) -> p t d", t=NQ)).then_inc(s_out, 16)
                    elif name == "cload":
                        atleast(sp, mix_step, MIX * a)
                        sp.dma_start(x_c, x_rows[a]).then_inc(c_in, 16)
                        sp.dma_start(xn_c, xn_rows[a]).then_inc(c_in, 16)
                    elif name == "sload":
                        atleast(sp, mix_step, MIX * a)
                        sp.wait_ge(s_out, 16 * (a + 1))
                        sp.dma_start(s_c, s_rows[a]).then_inc(s_in, 16)
                    elif name == "out":
                        sp.wait_ge(mix_step, MIX * (a + 1))
                        sp.dma_start(out_rows[a], t_c).then_inc(out_done, 16)
            sp.wait_ge(out_done, 16 * B)
            sp.wait_ge(xn_out, 16 * B)
            for s in range(FBUF):
                sp.wait_ge(y_out[s], 16 * (NF // FBUF))

        @block.gpsimd
        def _(pool):
            n_made = [0]

            def made(ins):
                n_made[0] += 1
                ins.then_inc(consts_made, 1)
                return n_made[0]

            nc.gpsimd.memset(ident[:, :], 0.0).then_inc(ident_made, 1)
            pool.wait_ge(ident_made, 1)
            nc.gpsimd.affine_select(out=ident[:, :], in_=ident[:, :], compare_op=ALU.not_equal, fill=1.0,
                                    base=0, pattern=[[-1, P]], channel_multiplier=1).then_inc(ident_made, 1)
            nc.gpsimd.memset(zero, 0.0).then_inc(zeroed, 1)
            made(nc.gpsimd.memset(mask2[:, :, :], 0.0))
            made(nc.gpsimd.memset(ltri[:, :], 1.0))
            made(nc.gpsimd.memset(onesb[:, :], 1.0))
            b = made(nc.gpsimd.memset(ones3[:, :], 1.0))
            pool.wait_ge(consts_made, b)
            made(nc.gpsimd.affine_select(out=mask2[:, :, :], in_=mask2[:, :, :], compare_op=ALU.is_ge, fill=MASKED,
                                         base=0, pattern=[[0, 2], [-1, P]], channel_multiplier=1))
            made(nc.gpsimd.affine_select(out=ltri[:, :], in_=ltri[:, :], compare_op=ALU.is_gt, fill=0.0,
                                         base=0, pattern=[[1, P]], channel_multiplier=-1))
            pool.wait_ge(ident_made, 2)
            made(nc.gpsimd.tensor_copy(identb[:, :], ident[:, :]))
            made(nc.gpsimd.iota(desc, pattern=[[-1, E]], base=E, channel_multiplier=0, allow_small_or_imprecise_dtypes=True))
            made(nc.gpsimd.iota(jot, pattern=[[P, NT]], base=0, channel_multiplier=0, allow_small_or_imprecise_dtypes=True))
            made(nc.gpsimd.iota(tio, pattern=[[1, NF]], base=0, channel_multiplier=0, allow_small_or_imprecise_dtypes=True))
            made(nc.gpsimd.memset(onef, 1.0))
            assert n_made[0] == CONSTS
            for n, t in enumerate(ks + qs):
                nc.gpsimd.memset(t[:, :, :].bitcast(F32), 0.0).then_inc(stacks_made, 1)
            nc.gpsimd.memset(vs[:, :, :, :], 0.0).then_inc(stacks_made, 1)
            pool.wait_ge(stacks_made, 5)
            for t in ks:
                nc.gpsimd.memset(t[MROW:P, :, :], 1.0).then_inc(stacks_made, 1)
            pool.wait_ge(stacks_made, 7)
            nc.gpsimd.memset(vs[:, :, :, DH:DH + 1], 1.0).then_inc(stacks_made, 1)
            assert STACK_SETS == 8

            for i, k, events in steps():
                for name, a in events:
                    if name == "sel":
                        b, j = a
                        pool.wait_ge(exp_done, st_units(b, UNITS * (j + 1) - 1))
                        h0 = 2 * j % HG
                        heads = probs[:, j // 2 % 2, h0:h0 + 2, :]
                        for blk in (every_512(heads[:, 0, :]), every_512(heads[:, 1, :]), heads[:, :, PT_AT[1]:PT_AT[1] + P]):
                            nc.gpsimd.affine_select(out=blk, in_=blk, compare_op=ALU.is_ge, fill=0.0, base=0,
                                                    pattern=[[0, blk.shape[1]], [1, P]],
                                                    channel_multiplier=-1).then_inc(selected, 1)
                    elif name == "sum":
                        pool.wait_ge(roped, NTH["Q", (a, 3)])
                        nc.gpsimd.tensor_tensor(qk[:, :, :], qk[:, :, :], qk_sin[:, :, :], ALU.add).then_inc(qk_sum, 1)
                    elif name == "rest":
                        pool.wait_ge(hi_done, NTH["hi", a])
                        nc.gpsimd.tensor_tensor(qk[:, :, :], qk[:, :, :], parts[:, :, 0, :], ALU.subtract).then_inc(rest_done, 1)
                    elif name == "low":
                        pool.wait_ge(mid_done, NTH["mid", a])
                        nc.gpsimd.tensor_tensor(parts[:, :, 2, :], qk[:, :, :], parts[:, :, 1, :], ALU.subtract).then_inc(low_done, 1)
                    elif name == "scatter":
                        if a == 0:
                            pool.wait_ge(routed, 1)
                            pool.wait_ge(rows_scaled, NT)
                            pool.wait_ge(zero_rows, 64)
                        s, t = a % 2, a // 2
                        nc.gpsimd.indirect_dma_start(
                            out=sorted_d, out_offset=bass.IndirectOffsetOnAxis(ap=index[:, s, t:t + 1], axis=0),
                            in_=xall[:, t, :], in_offset=None).then_inc(scattered, 16)
                    elif name == "gather":
                        c, r = a
                        if c == 0 and r == 0:
                            pool.wait_ge(scattered, 16 * 2 * NT)
                            for s in range(FBUF):
                                pool.wait_ge(y_out[s], 16 * (NF // FBUF))
                        if r == 0 and c >= 2:
                            pool.wait_ge(mix_step, MIX * (c - 1))
                        s, t = r // NQ, r % NQ
                        nc.gpsimd.indirect_dma_start(
                            out=y_in[c % 2][s][:, t, :], out_offset=None, in_=y_d,
                            in_offset=bass.IndirectOffsetOnAxis(ap=index[:, s, NQ * c + t:NQ * c + t + 1], axis=0)
                            ).then_inc(gathered[c % 2], 16)

        @block.scalar
        def _(act):
            act.wait_ge(r_dve, R_VAR)
            nc.scalar.activation(sq[:, :], va[:, :], ACT.Sqrt).then_inc(sq_done, 1)
            for b in range(B):
                act.wait_ge(xnT_ready, b + 1)
                nc.scalar.copy(xnT[:, b * S:(b + 1) * S], bank[:, b % 4, :]).then_inc(xnT_copied, 1)
                if b == 3:
                    act.wait_ge(r_dve, R_MS)
                    nc.scalar.activation(sq[:, :], va[:, :], ACT.Sqrt).then_inc(sq_done, 1)

            def exponentials(b, k):
                u, j = k % UNITS, k // UNITS
                g, h0 = j // 2, 2 * j % HG
                act.wait_ge(st_ready, st_units(b, k))
                if b == 0 and k == 0:
                    act.wait_ge(xnT_out, 16 * B)
                    act.wait_ge(zero_rows, 64)
                if j % 2 == 0 and u == 0 and (b > 0 or g >= 2):
                    act.wait_ge(pv_done, NTH["pv", (b - (g < 2), (g - 2) % NG, NQ - 1)])
                pt = probs[:, g % 2, :, :]
                src = bank[:, ST_BANK[k % 2], :]
                if u == 4:
                    dst = pt[:, h0:h0 + 2, PT_AT[2]:PT_AT[2] + 256]
                    src = src.rearrange("p (h q) -> p h q", h=2)
                else:
                    lo = 512 * (u % 2)
                    dst = pt[:, h0 + u // 2, lo:lo + 512]
                nc.scalar.activation(dst, src, ACT.Exp, scale=float(DH) ** -0.5).then_inc(exp_done, 1)

            for i, k, events in steps():
                if 0 <= i < B:
                    exponentials(i, k)
                for name, a in events:
                    if name == "oc":
                        b, g = a
                        act.wait_ge(pv_done, NTH["pv", (b, g, NQ - 1)])
                        atleast(act, ready["OT"], NTH["oc", a] - 1)
                        nc.scalar.copy(o_sb[:, :], bank[:, PV_BANK, :]).then_inc(o_copied, 1)
                    elif name == "V":
                        act.wait_ge(ready["V"], NTH["V", a])
                        if a == 0:
                            act.wait_ge(stacks_made, STACK_SETS)
                        else:
                            act.wait_ge(pv_done, NTH["pv", (a - 1, NG - 1, NQ - 1)])
                        nc.scalar.copy(vs[:, :, :, 0:DH], ring_bank((name, a)).rearrange("p (k h d) -> p k h d", k=NQ, h=H)
                                       ).then_inc(v_copied, 1)
                    elif name == "mT":
                        b, f = a
                        act.wait_ge(ready["mT"], NTH["mT", a])
                        atleast(act, m_written[f], 16 * b)
                        nc.scalar.copy(mT[:, f, :], ring_bank((name, a))[0:3 * HALF, 0:256].bitcast(BF16)).then_inc(mT_copied, 1)
                    elif name == "hi":
                        act.wait_ge(qk_sum, NTH["sum", a])
                        atleast(act, parts_out, 16 * a)
                        nc.scalar.copy(parts[:, :, 0, :], qk[:, :, :]).then_inc(hi_done, 1)
                    elif name == "mid":
                        act.wait_ge(rest_done, NTH["rest", a])
                        nc.scalar.copy(parts[:, :, 1, :], qk[:, :, :]).then_inc(mid_done, 1)
                    elif name == "e2":
                        act.wait_ge(r_dve, R_TOP)
                        nc.scalar.activation(e2, e2, ACT.Exp).then_inc(e2_done, 1)
                    elif name == "AT":
                        act.wait_ge(ready["AT"], NTH["AT", a])
                        atleast(act, ready["WO"], a)
                        nc.scalar.copy(actsT[:, :], ring_bank((name, a))).then_inc(aT_copied, 1)
                    elif name == "WO":
                        act.wait_ge(ready["WO"], NTH["WO", a])
                        nc.scalar.copy(s_sb[:, :], ring_bank((name, a))).then_inc(s_copied, 1)
                    elif name == "F":
                        act.wait_ge(ready["F"], a + 1)
                        if a >= 2 * FBUF:
                            act.wait_ge(y_out[a % FBUF], 16 * (a // FBUF - 1))
                        cols = slot_columns(a)
                        nc.scalar.copy(slot[:, a % FBUF, cols], ring_bank((name, a))[:, cols]).then_inc(slot_copied, 1)
                    elif name == "tanh":
                        act.wait_ge(halves_read, 2 * a + 1)
                        atleast(act, prod_done, a - 1)
                        nc.scalar.activation(tanh_g[:, a % 2, :], glu[:, a % 2, :], ACT.Tanh, scale=ALPHA / 2).then_inc(tanh_done, 1)
                    elif name == "mtanh":
                        act.wait_ge(mix_step, MIX * a + 4)
                        nc.scalar.activation(y_in[a % 2][1], y_in[a % 2][0], ACT.Tanh, scale=0.5).then_inc(mix_tanh, 1)

        @block.vector
        def _(dve):
            n_r = [0]

            def link(ins):
                n_r[0] += 1
                ins.then_inc(r_dve, 1)
                dve.wait_ge(r_dve, n_r[0])

            v = nc.vector
            for t in range(NT):
                if t % NQ == 0:
                    dve.wait_ge(x_in[t // NQ], 16)
                ins = v.bn_stats(stats[:, t, :], xall[:, t, :])
            link(ins)
            for t in range(NT):
                ins = v.bn_aggr(mv[:, t, :], stats[:, t, :])
            link(ins)
            link(v.tensor_scalar(va[:, :], mv[:, :, 1], EPS, None, ALU.add))
            assert n_r[0] == R_VAR

            def rsqrt(dst, n_act):
                dve.wait_ge(sq_done, n_act)
                link(v.reciprocal(dst, sq[:, :]))
                link(v.tensor_tensor(rt[:, :], dst, dst, ALU.mult))
                link(v.tensor_tensor(rt[:, :], rt[:, :], va[:, :], ALU.mult))
                link(v.tensor_scalar(rt[:, :], rt[:, :], -0.5, 1.5, ALU.mult, ALU.add))
                link(v.tensor_tensor(dst, dst, rt[:, :], ALU.mult))
            rsqrt(rs[:, :], 1)
            link(v.tensor_tensor(rt[:, :], rs[:, :], rs[:, :], ALU.mult))
            link(v.tensor_tensor(rt[:, :], rt[:, :], mv[:, :, 1], ALU.mult))
            link(v.tensor_scalar(va[:, :], rt[:, :], EPS, None, ALU.add))
            assert n_r[0] == R_MS
            for t in range(NT):
                v.tensor_scalar(xall[:, t, :], xall[:, t, :], mv[:, t, 0:1], rs[:, t:t + 1],
                                ALU.subtract, ALU.mult).then_inc(rows_ready, 1)
            v.memset(bank[:, PV_BANK, :], 0.0).then_inc(pv_zeroed, 1)
            dve.wait_ge(small_in, 16 * SMALL_LOADS)
            link(v.tensor_scalar(gate[:, :], gate[:, :], scale[:, 0:1], None, ALU.mult))
            assert n_r[0] == R_GATE
            rsqrt(rr[:, :], 2)

            def te(ap):
                return ap.rearrange("p (t e) -> p t e", e=E)

            def et(ap):
                return ap.rearrange("p (e t) -> p e t", e=E)

            def over_e(ap):
                return ap.unsqueeze(2).to_broadcast([P, NT, E])

            def over_t(ap):
                return ap.unsqueeze(1).to_broadcast([P, NT, E])

            def top(vm, oh):
                link(v.tensor_reduce(vm, te(lg), AX.X, ALU.max))
                link(v.tensor_tensor(te(sc1), te(lg), over_e(vm), ALU.is_ge))
                link(v.tensor_tensor(te(sc1), te(sc1), over_t(desc), ALU.mult))
                link(v.tensor_reduce(idf, te(sc1), AX.X, ALU.max))
                link(v.tensor_tensor(te(oh), over_t(desc), over_e(idf), ALU.is_equal))

            def route():
                dve.wait_ge(logits_ready, 1)
                dve.wait_ge(consts_made, CONSTS)
                link(v.tensor_tensor(te(lg), te(bank[:, LOGIT_BANK, 0:NE]), over_e(rr[:, :]), ALU.mult))
                link(v.tensor_tensor(te(lg), te(lg), over_t(gate_b[:, :]), ALU.add))
                top(v1, oh1)
                link(v.scalar_tensor_tensor(te(lg), te(oh1), MASKED, te(lg), ALU.mult, ALU.add))
                top(v2, oh2)
                link(v.tensor_tensor(cbf, oh1, oh2, ALU.add))
                assert n_r[0] == R_CNT
                link(v.tensor_tensor(e2, v2, v1, ALU.subtract))
                assert n_r[0] == R_TOP
                dve.wait_ge(ranks_ready, 1)
                link(v.tensor_copy(et(tot), bank[:, RANK_BANK, NE:2 * NE].rearrange("p (t e) -> p e t", e=E)))
                for e in range(E):
                    ins = v.tensor_tensor_scan(et(inc)[:, e, :], onef, et(tot)[:, e, :], 0.0, ALU.mult, ALU.add)
                link(ins)
                link(v.tensor_tensor(et(cmpj), et(inc)[:, :, NT - 1:NT].to_broadcast([P, E, NT]),
                                     jot.unsqueeze(1).to_broadcast([P, E, NT]), ALU.is_gt))
                link(v.tensor_reduce(nte[:, 0:E], et(cmpj), AX.X, ALU.add))
                link(v.tensor_tensor_scan(cn[:, 0:E], onef[:, 0:E], nte[:, 0:E], 0.0, ALU.mult, ALU.add))
                link(v.tensor_tensor(start8, cn[:, 0:E], nte[:, 0:E], ALU.subtract))
                link(v.tensor_tensor(et(inc), et(inc), et(tot), ALU.subtract))
                link(v.tensor_tensor(te(posb), te(bank[:, RANK_BANK, 0:NE]), et(inc).rearrange("p e t -> p t e"), ALU.add))
                assert n_r[0] == R_RANKS
                link(v.scalar_tensor_tensor(te(posb), over_t(start8), float(P), te(posb), ALU.mult, ALU.add))
                for s, oh in enumerate((oh1, oh2)):
                    link(v.tensor_tensor(sc2, oh, posb, ALU.mult))
                    link(v.tensor_reduce(idf, te(sc2), AX.X, ALU.add))
                    link(v.tensor_copy(index[:, s, :], idf))
                e_cmp = ecmp[0:1, :].rearrange("p (t e) -> p t e", e=E)
                link(v.tensor_tensor(e_cmp, tio[0:1, :].unsqueeze(2).to_broadcast([1, NF, E]),
                                     cn[0:1, 0:E].unsqueeze(1).to_broadcast([1, NF, E]), ALU.is_ge))
                link(v.tensor_reduce(esum[0:1, :], e_cmp, AX.X, ALU.add))
                v.tensor_scalar(expert[:, :], esum[0:1, :], float(E - 1), None, ALU.min).then_inc(routed, 1)

            def row_maxima(b, k):
                u, j = k % UNITS, k // UNITS
                hd = 2 * j + u // 2
                dve.wait_ge(s_ready, st_units(b, k))
                src = bank[:, S_BANK[k % 2], :]
                if u == 4:
                    ins = v.tensor_reduce(rowmax[:, 1, 2 * j:2 * j + 2], src.rearrange("p (h k) -> p h k", h=2), AX.X, ALU.max)
                elif u % 2 == 0:
                    ins = v.tensor_reduce(rowmax[:, 3, hd:hd + 1], src, AX.X, ALU.max)
                else:
                    v.tensor_reduce(rowmax[:, 2, hd:hd + 1], src[:, 0:384], AX.X, ALU.max)
                    ins = v.tensor_reduce(rowmax[:, 0, hd:hd + 1], src[:, 384:512], AX.X, ALU.max)
                ins.then_inc(max_done, 1)

            for i, k, events in steps():
                if -1 <= i < B - 1:
                    row_maxima(i + 1, k)
                for name, a in events:
                    if name == "msplit":
                        b, f = a
                        done = 4 * (NTH["msplit", a] - 1)
                        dve.wait_ge(max_done, st_units(b, STEPS // 2 * (f + 1) - 1))
                        if b > 0:
                            dve.wait_ge(ready["mT"], NTH["mT", (b - 1, f)])
                        mx = rowmax[:, :, f * HALF:(f + 1) * HALF]
                        nm = msplit[:, f, :, :, :]
                        v.tensor_scalar(nm[:, :, 0, :], mx, -1.0, None, ALU.mult).then_inc(split_done, 1)
                        dve.wait_ge(split_done, done + 1)
                        v.scalar_tensor_tensor(mrest[:, :, :], mx, -1.0, nm[:, :, 0, :], ALU.mult, ALU.subtract).then_inc(split_done, 1)
                        dve.wait_ge(split_done, done + 2)
                        v.tensor_copy(nm[:, :, 1, :], mrest[:, :, :]).then_inc(split_done, 1)
                        dve.wait_ge(split_done, done + 3)
                        v.tensor_tensor(nm[:, :, 2, :], mrest[:, :, :], nm[:, :, 1, :], ALU.subtract).then_inc(split_done, 1)
                    elif name == "route":
                        route()
                    elif name == "rowt":
                        dve.wait_ge(xn_out, 16 * B)
                        dve.wait_ge(xnT_ready, B)
                        for t in range(NT):
                            v.tensor_scalar(xall[:, t, :], xall[:, t, :], rr[:, t:t + 1], None, ALU.mult).then_inc(rows_scaled, 1)
                    elif name == "weigh":
                        dve.wait_ge(e2_done, 1)
                        link(v.tensor_scalar(p1, e2, 1.0, None, ALU.add))
                        link(v.reciprocal(p1, p1))
                        link(v.tensor_scalar(wts[:, 0, :], p1, 0.5, None, ALU.mult))
                        link(v.tensor_tensor(wts[:, 1, :], wts[:, 0, :], e2, ALU.mult))
                    elif name == "bias":
                        dve.wait_ge(big_in, 32)
                        link(v.tensor_scalar(w1[:, :], w1[:, :], scale[:, 0:1], None, ALU.mult))
                        link(v.tensor_scalar(braw[:, 32:40], braw[:, 32:40], 2.0, None, ALU.mult))
                        link(v.tensor_copy(bparts[:, 0, :], braw[:, :]))
                        link(v.tensor_tensor(braw[:, :], braw[:, :], bparts[:, 0, :], ALU.subtract))
                        link(v.tensor_copy(bparts[:, 1, :], braw[:, :]))
                        v.tensor_tensor(bparts[:, 2, :], braw[:, :], bparts[:, 1, :], ALU.subtract).then_inc(weights_made, 1)
                    elif name == "Q":
                        b, c = a
                        dve.wait_ge(ready["Q"], NTH["Q", a])
                        if c == 0:
                            atleast(dve, low_done, b)
                        dst, tab = ((qk, cos), (qk_sin, sin))[c % 2]
                        v.tensor_tensor(dst[:, c // 2, :], ring_bank((name, a)), tab[:, :], ALU.mult).then_inc(roped, 1)
                    elif name == "H":
                        src = ring_bank((name, a))
                        dve.wait_ge(ready["H"], a + 1)
                        v.tensor_scalar(glu[:, a % 2, :], src[:, 0:I], LIMIT, None, ALU.min).then_inc(halves_read, 1)
                        v.tensor_scalar(lin[:, a % 2, :], src[:, I:2 * I], LIMIT, -LIMIT, ALU.min, ALU.max).then_inc(halves_read, 1)
                    elif name == "glu":
                        dve.wait_ge(tanh_done, a + 1)
                        v.scalar_tensor_tensor(glu[:, a % 2, :], tanh_g[:, a % 2, :], 1.0, glu[:, a % 2, :],
                                               ALU.add, ALU.mult).then_inc(prod_done, 1)
                        dve.wait_ge(prod_done, a + 1)
                        v.scalar_tensor_tensor(hid[:, a % 2, :], lin[:, a % 2, :], 1.0, glu[:, a % 2, :],
                                               ALU.add, ALU.mult).then_inc(hid_done, 1)
                    elif name == "OT":
                        b, g = a
                        dve.wait_ge(ready["OT"], NTH["OT", a])
                        o4 = ring_bank((name, a)).rearrange("p (t c r) -> p t c r", t=NQ, c=HG)
                        v.reciprocal(recip[:, :, :], o4[:, :, :, DH]).then_inc(recip_done, 1)
                        dve.wait_ge(recip_done, NTH["OT", a])
                        atleast(dve, s_out, 16 * b)
                        dst = acts[:, :].rearrange("p (t g c d) -> p t g c d", t=NQ, g=NG, c=HG)[:, :, g, :, :]
                        v.tensor_tensor(dst, o4[:, :, :, 0:DH], recip[:, :, :].unsqueeze(3).to_broadcast([P, NQ, HG, DH]),
                                        ALU.mult).then_inc(acts_done, 1)
                    elif name == "mix":
                        c, m = a
                        y1, y2 = y_in[c % 2]
                        if m in (0, 1):
                            wt = wts[:, m, NQ * c:NQ * (c + 1)].unsqueeze(2).to_broadcast([P, NQ, D])
                            dve.wait_ge(gathered[c % 2], 16 * 2 * NQ * (c // 2 + 1))
                            ins = v.tensor_tensor((y1, y2)[m], (y1, y2)[m], wt, ALU.mult)
                        else:
                            dve.wait_ge(mix_step, MIX * c + m)
                        if m == 2:
                            ins = v.tensor_tensor(y1, y1, y2, ALU.add)
                        elif m == 3:
                            dve.wait_ge(c_in, 32 * (c + 1))
                            ins = v.tensor_tensor(y1, y1, xn_c, ALU.add)
                        elif m == 4:
                            dve.wait_ge(mix_tanh, c + 1)
                            ins = v.scalar_tensor_tensor(y1, y2, 1.0, y1, ALU.add, ALU.mult)
                        elif m == 5:
                            dve.wait_ge(s_in, 16 * (c + 1))
                            ins = v.tensor_tensor(y1, y1, s_c, ALU.mult)
                        elif m == 6:
                            atleast(dve, out_done, 16 * c)
                            ins = v.scalar_tensor_tensor(t_c, y1, 0.5, x_c, ALU.mult, ALU.add)
                        ins.then_inc(mix_step, 1)

        @block.tensor
        def _(pe):
            pe.wait_ge(ident_made, 2)
            for b in range(B):
                pe.wait_ge(rows_ready, NQ * (b + 1))
                if b >= 4:
                    pe.wait_ge(xnT_copied, b - 3)
                for t in range(NQ):
                    ins = nc.tensor.transpose(bank[:, b % 4, P * t:P * (t + 1)], xall[:, NQ * b + t, :], ident[:, :])
                ins.then_inc(xnT_ready, 1)

            def score_keys_by_queries(b, k):
                u, j, par = k % UNITS, k // UNITS, b % 2
                ha, hb = 2 * j, 2 * j + 1
                if k in (0, STEPS // 2):
                    pe.wait_ge(m_in[k // (STEPS // 2)], 16 * (b + 1))
                atleast(pe, exp_done, st_units(b, k) - 2)
                out = bank[:, ST_BANK[k % 2], :]
                todo = {0: ((ha, 0, 0),), 1: ((ha, 3, 0), (ha, 1, 128)), 2: ((hb, 0, 0),), 3: ((hb, 3, 0), (hb, 1, 128)),
                        4: ((ha, 2, 0), (hb, 2, 256))}[u]
                for h, kt, col in todo:
                    n = S - P * kt
                    ins = nc.tensor.matmul(out[:, col:col + n], ks[par][:, h, P * kt:P * (kt + 1)],
                                           qs[par][:, h, P * kt:S], start=True, stop=True)
                ins.then_inc(st_ready, 1)

            def score_queries_by_keys(b, k):
                u, j, par = k % UNITS, k // UNITS, b % 2
                ha, hb = 2 * j, 2 * j + 1
                if k in (0, STEPS // 2):
                    pe.wait_ge(stack_in[b % 2][k // (STEPS // 2)], STACK_LOADS * 16 * (b // 2 + 1))
                if b == 0 and k == 0:
                    pe.wait_ge(r_dve, R_RANKS)
                atleast(pe, max_done, st_units(b, k) - 2)
                out = bank[:, S_BANK[k % 2], :]
                todo = {0: ((ha, 3, 0),), 1: ((ha, 2, 0), (ha, 0, 384)), 2: ((hb, 3, 0),), 3: ((hb, 2, 0), (hb, 0, 384)),
                        4: ((ha, 1, 0), (hb, 1, 256))}[u]
                for n, (h, qt, col) in enumerate(todo):
                    w = P * (qt + 1)
                    nc.tensor.matmul(out[:, col:col + w], qs[par][0:MROW, h, P * qt:P * (qt + 1)],
                                     ks[par][0:MROW, h, 0:w], start=(n == 0), stop=False, skip_group_check=True)
                if u == 4:
                    dst, m = out.rearrange("p (h k q) -> p h k q", h=2, k=2)[:, :, 1, :], mask2[:, :, :]
                elif u % 2:
                    dst, m = out[:, 256:512].rearrange("p (k q) -> p k q", k=2), mask2[:, :, :]
                else:
                    dst, m = out[:, 384:512], mask2[:, 0, :]
                nc.tensor.matmul(dst, identb[:, :], m, start=False, stop=True, skip_group_check=True).then_inc(s_ready, 1)

            chosen = {}
            for i, k, events in steps():
                if 0 <= i < B:
                    score_keys_by_queries(i, k)
                if -1 <= i < B - 1:
                    score_queries_by_keys(i + 1, k)
                for name, a in events:
                    if name == "logits":
                        pe.wait_ge(xnT_copied, B)
                        pe.wait_ge(r_dve, R_GATE)
                        for t in range(NT):
                            ins = nc.tensor.matmul(bank[:, LOGIT_BANK, E * t:E * (t + 1)], xnT[:, P * t:P * (t + 1)], gate[:, :],
                                                   start=True, stop=True)
                        ins.then_inc(logits_ready, 1)
                    elif name == "rank":
                        pe.wait_ge(r_dve, R_CNT)
                        nc.tensor.matmul(bank[:, RANK_BANK, 0:NE], ltri[:, :], cbf, start=True, stop=True)
                        nc.tensor.matmul(bank[:, RANK_BANK, NE:2 * NE], onesb[:, :], cbf, start=True, stop=True).then_inc(ranks_ready, 1)
                    elif name == "pv":
                        b, g, kt = a
                        if kt == 0:
                            pe.wait_ge(selected, SELECTS * NTH["sel", (b, 2 * g + 1)])
                            atleast(pe, o_copied, NTH["oc", (b, g)] - 1)
                            if g == 0:
                                pe.wait_ge(v_copied, b + 1)
                                if b == 0:
                                    pe.wait_ge(pv_zeroed, 1)
                        w = S - P * kt
                        for c in range(HG):
                            ins = nc.tensor.matmul(bank[32 * c:32 * c + VC, PV_BANK, P * kt:S], vs[:, kt, HG * g + c, :],
                                                   probs[:, g % 2, c, PT_AT[kt]:PT_AT[kt] + w],
                                                   start=(kt == 0), stop=(kt == NQ - 1), skip_group_check=True)
                        ins.then_inc(pv_done, 1)
                    if name not in RING:
                        continue
                    if RING_AT[name, a] >= 3:
                        before = RING_USERS[RING_AT[name, a] - 3]
                        seen, signals = reader[before[0]]
                        pe.wait_ge(seen, signals * NTH[before])
                    dst = ring_bank((name, a))
                    if name == "Q":
                        b, c = a
                        if b < 2:
                            pe.wait_ge(xnT_copied, b + 1)
                            if b == 0 and c == 0:
                                pe.wait_ge(small_in, 16 * SMALL_LOADS)
                            src = xnT[:, b * S:(b + 1) * S]
                        else:
                            pe.wait_ge(xq_in, 16 * NTH["xq", b])
                            src = xp[:, :]
                        ins = nc.tensor.matmul(dst, wq[:, P * c:P * (c + 1)], src, start=True, stop=True)
                    elif name == "V":
                        pe.wait_ge(xv_in, 16 * (a + 1))
                        for t in range(NQ):
                            ins = nc.tensor.matmul(dst[:, P * t:P * (t + 1)], xp[:, P * t:P * (t + 1)], wv[:, :], start=True, stop=True)
                    elif name == "mT":
                        pe.wait_ge(split_done, 4 * NTH["msplit", a])
                        for t in range(NQ):
                            ins = nc.tensor.transpose(dst.bitcast(BF16)[0:3 * HALF, P * t:P * (t + 1)],
                                                      msplit[:, a[1], t, :, :].rearrange("p c h -> p (c h)"), identb[:, :])
                    elif name == "OT":
                        pe.wait_ge(o_copied, NTH["oc", a])
                        for t in range(NQ):
                            ins = nc.tensor.transpose(dst[:, P * t:P * (t + 1)], o_sb[:, P * t:P * (t + 1)], ident[:, :])
                    elif name == "AT":
                        pe.wait_ge(acts_done, NTH["OT", (a, NG - 1)])
                        for t in range(NQ):
                            ins = nc.tensor.transpose(dst[:, P * t:P * (t + 1)], acts[:, P * t:P * (t + 1)], ident[:, :])
                    elif name == "WO":
                        pe.wait_ge(aT_copied, a + 1)
                        for t in range(NQ):
                            ins = nc.tensor.matmul(dst[:, P * t:P * (t + 1)], actsT[:, P * t:P * (t + 1)], wo[:, :], start=True, stop=True)
                    elif name == "F":
                        if a == 0:
                            pe.wait_ge(routed, 1)
                            pe.wait_ge(weights_made, 1)
                            pe.wait_ge(bias_in, 16)
                        if a >= 3:
                            pe.wait_ge(slot_copied, a)
                            e = chosen.pop(a - 3)
                            hT = slot[:, (a - 1) % FBUF, HID_AT]
                            for c in range(2):
                                nc.tensor.matmul(dst[:, Y_AT], hT[:, P * c:P * (c + 1)], w2[:, bass.ds(e * (2 * D) + c * D, D)],
                                                 start=(c == 0), stop=False)
                            ins = nc.tensor.matmul(dst[:, Y_AT], ones3[:, :], bias[:, bass.ds(e * D + E * 2 * I, D)], start=False, stop=True)
                        if 2 <= a < NF + 2:
                            pe.wait_ge(hid_done, a - 1)
                            for c in range(2):
                                ins = nc.tensor.transpose(dst[:, P * (c + 1):P * (c + 2)], hid[:, a % 2, P * c:P * (c + 1)], ident[:, :])
                        if a < NF:
                            pe.wait_ge(xs_in[a % XBUF], 16 * (a // XBUF + 1))
                            ins = nc.tensor.transpose(dst[:, X_AT], xs[:, a % XBUF, :], ident[:, :])
                    elif name == "H":
                        pe.wait_ge(slot_copied, a + 1)
                        e = pe.value_load(expert[0:1, a:a + 1], min_val=0, max_val=E - 1)
                        chosen[a] = e
                        nc.tensor.matmul(dst, slot[:, a % FBUF, X_AT], w1[:, bass.ds(e * (2 * I), 2 * I)], start=True, stop=False)
                        ins = nc.tensor.matmul(dst, ones3[:, :], bias[:, bass.ds(e * (2 * I), 2 * I)], start=False, stop=True)
                    ins.then_inc(ready[name], 1)


SMALL_LOADS, STACK_LOADS = 10, 9
CONSTS, STACK_SETS = 11, 8
R_VAR, R_MS, R_GATE, R_CNT, R_TOP, R_RANKS = 3, 11, 12, 31, 32, 40


def slot_columns(n):
    return slice(0 if n < NF else P if n < NF + 2 else 3 * P, P if n < 2 else 3 * P if n < 3 else 4 * P)


def rope_tables():
    inv = (1.0 / np.float32(THETA) ** (np.arange(0, DH, 2, dtype=np.float32) / np.float32(DH))).astype(np.float32)
    f = np.arange(S, dtype=np.float32)[None, :] * inv[:, None]
    cos, sin = np.cos(f.astype(np.float64)), np.sin(f.astype(np.float64))
    cos = np.repeat(cos, 2, axis=0)
    sin = np.stack([-sin, sin], axis=1).reshape(DH, S)
    return tuple(np.ascontiguousarray(np.repeat(t, H, axis=0).astype(np.float32)) for t in (cos, sin))


def kernel(L0_attn_X, L0_attn_W_KQV, L0_attn_W_O, L0_ffn_norm_scale, L0_ffn_gate_w, L0_ffn_gate_b,
           L0_ffn_mlp1_w, L0_ffn_mlp1_b, L0_ffn_mlp2_w, L0_ffn_mlp2_b):
    import concourse.bacc as _bacc
    from concourse.bass_utils import run_bass_kernel_spmd as _run

    c = np.ascontiguousarray
    wt = np.asarray(L0_attn_W_KQV)
    order = np.array([h * DH + d for d in range(DH) for h in range(H)])
    swapped = np.array([h * DH + (d ^ 1) for d in range(DH) for h in range(H)])
    wk, wqm, wvm = wt[0:D], wt[D:2 * D], wt[2 * D:3 * D]
    wq = np.concatenate([wqm[order], wqm[swapped], wk[order], wk[swapped]], axis=0).T
    w1 = np.asarray(L0_ffn_mlp1_w).reshape(E, D, I, 2).transpose(1, 0, 3, 2).reshape(D, E * 2 * I)
    b1 = np.asarray(L0_ffn_mlp1_b).reshape(E, I, 2).transpose(0, 2, 1).reshape(P, E * 2 * I // P)
    w2 = np.asarray(L0_ffn_mlp2_w).reshape(E, 2, P, D).transpose(2, 0, 1, 3).reshape(P, E * 2 * D)
    cos, sin = rope_tables()
    arrays = {
        "x": np.asarray(L0_attn_X).reshape(B * S, D), "wq": wq, "wv": wvm.T, "wo": np.asarray(L0_attn_W_O).T,
        "cos_t": cos, "sin_t": sin, "norm_scale": np.asarray(L0_ffn_norm_scale).reshape(D, 1),
        "gate_w": np.asarray(L0_ffn_gate_w), "gate_bias": np.asarray(L0_ffn_gate_b).reshape(1, E),
        "w1_t": w1, "b1_t": b1, "w2_t": w2, "b2_t": np.asarray(L0_ffn_mlp2_b).reshape(P, E * D // P),
    }
    arrays = {n: c(a) for n, a in arrays.items()}
    nc = _bacc.Bacc("TRN2", target_bir_lowering=False, num_devices=1)
    aps = [nc.dram_tensor("in_" + n, a.shape, mybir.dt.from_np(a.dtype), kind="ExternalInput").ap() for n, a in arrays.items()]
    out = nc.dram_tensor("out", (B * S, D), F32, kind="ExternalOutput").ap()
    build(nc, *aps, out)
    r = _run(nc, [{"in_" + n: a for n, a in arrays.items()}], core_ids=[0])
    return r.results[0]["out"].reshape(B, S, D)
```

```python
from contextlib import ExitStack

import numpy as np

import concourse.bass as bass
from concourse import mybir

F32 = mybir.dt.float32
BF16 = mybir.dt.bfloat16
I32 = mybir.dt.int32
U32 = mybir.dt.uint32
ALU = mybir.AluOpType
ACT = mybir.ActivationFunctionType
AX = mybir.AxisListType

P = 128
B, S, D = 8, 512, 128
H, DH = 16, 8
E, I = 8, 256
NQ = S // P
NT = B * NQ
HG = 4
NG = H // HG
HALF = H // 2
VC = 16
LIMIT, ALPHA, EPS, THETA = 7.0, 1.702, 1e-5, 10000.0
MASKED = -1e30

K_PART = (0, 0, 0, 1, 1, 2)
Q_PART = (0, 1, 2, 0, 1, 0)
MROW = 96

PT_AT = (0, 640, 1024, 512)
PT_COLS = 1280
UNITS = 5
STEPS = UNITS * H // 2

W1_AT, W2_AT, B2_AT, B1_AT = 0, 2 * I, 2 * I + 2 * D, 2 * I + 2 * D + D // 2
W_COLS = B1_AT + 8
GLU_B, LIN_LO, LIN_HI, LIN_B = (B1_AT + 2 * n for n in range(4))

NF = (B * S * 2) // P + E
LAG = 3
XBUF, FBUF, HBUF, WBUF = 6, 3, LAG, LAG + 1
CUT_BY_DVE = (2,)
MASKED_BY_PE = (0, 6, 7)
H_AT, TANH_AT, LIFT_AT, GLU_AT = 2, 4, 4, 6
XLOAD_AHEAD = 5
IN_6, SPACING = 4, 9
SELECTS = 3


def every_512(head):
    return bass.AP(tensor=head.tensor, offset=head.offset, ap=[head.ap[0], [512, 3], [1, P]])


def timeline():
    at = {i: [[] for _ in range(STEPS)] for i in range(-2, B + 2)}

    def put(i, k, name, which):
        at[i + k // STEPS][k % STEPS].append((name, which))

    def first(i, k, name, which):
        at[i + k // STEPS][k % STEPS].insert(0, (name, which))

    for b in range(B):
        i = b - 2
        q0 = 11 if i >= 0 else 1
        if b >= 2:
            put(i, q0 - 3, "xq", b)
        for c in range(4):
            put(i, q0 + c, "Q", (b, c))
        for name, k in (("sum", 4), ("hi", 5), ("rest", 7), ("mid", 8), ("low", 10)):
            put(i, q0 + k, name, b)
        put(i, 24 if b == 1 else q0 + 11, "parts", b)
        put(i, 25 if b != 0 else q0 + 12, "stack", (b, 0))
        put(i, 39 if b > 1 else 26 if b == 1 else q0 + 13, "stack", (b, 1))
        for f in range(2):
            k = 20 * (f + 1)
            put(b - 1, k, "msplit", (b, f))
            put(b - 1, k + 2, "mT", (b, f))
            put(b - 1, k + 2, "mout", (b, f))
            put(b - 1, k + 4, "min", (b, f))
        put(b - 1, 30, "xv", b)
        put(b, 7, "V", b)
        for j in range(H // 2):
            if b not in MASKED_BY_PE:
                put(b, 5 * j + 5, "sel", (b, j))
        for g in range(NG):
            for kt in range(NQ):
                put(b, 10 * g + 12 + kt, "pv", (b, g, kt))
            put(b, 10 * g + 16, "oc", (b, g))
            put(b, 10 * g + 18, "OT", (b, g))
        put(b, 50, "AT", b)
        put(b, 52, "WO", b)
    put(-2, 5, "logits", 0)
    put(-2, 6, "rank", 0)
    put(-2, 6, "route", 0)
    put(-2, 39, "wload", 0)
    put(-2, 12, "rowt", 0)
    put(-2, 12, "clear", 0)
    put(-2, 14, "e2", 0)
    put(0, 8, "weigh", 0)
    for e in range(E):
        put(0, 20 + e, "w1", e)
    put(0, 29, "bias", 0)
    put(0, 31, "bload", 0)
    for n in range(2 * NT):
        m = n - SCATTER_FIRST
        put(-1 if m < 0 else 0, n + 5 if m < 0 else m, "scatter", n)
    for n in range(NF + LAG):
        i, k = 1 + n // SLOTS, (n % SLOTS) * STEPS // SLOTS
        if n < NF:
            put(i, k - XLOAD_AHEAD, "xload", n)
            put(i, k - 1, "wcopy", n)
            put(i, k + H_AT, "H", n)
            first(i, k + H_AT + 1, "H2", n)
            put(i, k + TANH_AT, "tanh", n)
            put(i, k + LIFT_AT, "lift", n)
            put(i, k + GLU_AT, "glu", n)
        put(i, k, "F", n)
        if n >= LAG:
            put(i, k + 1, "yout", n)
    for c in range(B):
        i, k = (6, 10 * c) if c < IN_6 else (7, SPACING * (c - IN_6))
        for r in range(2 * NQ):
            put(i, k + r, "gather", (c, r))
        put(i, k + 8, "cload", c)
        for m, d in enumerate((9, 10, 11, 12, 15)):
            put(i, k + d, "mix", (c, m))
        put(i, k + 14, "mtanh", c)
        late = k + 16 if c < B - 1 else (8 - i) * STEPS + 13
        if c < B - 1:
            put(i, k + 8, "sload", c)
        put(i, late, "mix", (c, 5))
        put(i, late + 1, "mix", (c, 6))
        put(i, late + 2, "out", c)
    return at


SLOTS = 15
SCATTER_FIRST = 34
TIMELINE = timeline()
RING = ("Q", "V", "F", "H", "OT", "mT", "AT", "WO")
YBUF = 3
MIX = 7


def ordinals():
    nth, count, ring = {}, {}, []
    for i, steps in TIMELINE.items():
        for step in steps:
            for name, which in step:
                count[name] = count.get(name, 0) + 1
                nth[name, which] = count[name]
                if name in RING:
                    ring.append((name, which))
    return nth, ring


NTH, RING_USERS = ordinals()
RING_AT = {user: n for n, user in enumerate(RING_USERS)}


def steps():
    for i, ks in TIMELINE.items():
        for k, events in enumerate(ks):
            yield i, k, events


def atleast(eng, sem, n):
    if n > 0:
        eng.wait_ge(sem, n)



def build(nc, x_h, wq_h, wv_h, wo_h, cos_h, sin_h, scale_h, gate_w_h, gate_b_h, w1_h, b1_h, w2_h, b2_h, out_h):
    ctx = ExitStack()
    with ctx:
        def sb(name, shape, dt=F32):
            return ctx.enter_context(nc.sbuf_tensor(name, shape, dt))

        def sem(name):
            return ctx.enter_context(nc.semaphore(name))

        xall = sb("xall", [P, NT, D])
        weights = sb("weights", [P, E, W_COLS])
        chosen = xall[:, :, :].rearrange("p t d -> p (t d)")[:, 0:WBUF * W_COLS].rearrange("p (n c) -> p n c", n=WBUF)
        w1, b1 = weights[:, :, W1_AT:W1_AT + 2 * I], weights[:, :, B1_AT:B1_AT + 4]
        b2 = weights[:, :, B2_AT:B1_AT].bitcast(BF16)
        wq, wv, wo = sb("wq", [P, 4 * P]), sb("wv", [P, D]), sb("wo", [P, D])
        cos, sin = sb("cos", [P, S]), sb("sin", [P, S])
        qs = [sb(f"qs{n}", [P, H, S], BF16) for n in range(2)]
        ks = [sb(f"ks{n}", [P, H, S], BF16) for n in range(2)]
        probs = sb("probs", [P, 2, HG, PT_COLS])
        vs = sb("vs", [P, NQ, H, VC])
        o_sb, acts, actsT = (sb(n, [P, S]) for n in ("o_sb", "acts", "actsT"))
        s_sb = acts
        qk = sb("qk", [P, 2, S])
        qk_sin = sb("qk_sin", [P, 2, S])
        parts = sb("parts", [P, 2, 3, S], BF16)
        xp = sb("xp", [P, S])
        xs = sb("xs", [P, XBUF, D])
        slot = sb("slot", [P, FBUF, 2 * P])
        glu, lin, tanh_g = (sb(n, [P, HBUF, I]) for n in ("glu", "lin", "tanh_g"))
        hid = lin
        rowmax = sb("rowmax", [P, NQ, H])
        msplit = sb("msplit", [P, 2, NQ, 3, HALF], BF16)
        mrest = sb("mrest", [P, NQ, HALF])
        mT = sb("mT", [3 * HALF, 2, S], BF16)
        recip = sb("recip", [P, NQ, HG])
        ident, identb = sb("ident", [P, P]), sb("identb", [P, P], BF16)
        mask2 = sb("mask2", [P, 2, P], BF16)
        ones3 = sb("ones3", [P, P], BF16)
        ltri, onesb = sb("ltri", [P, P], BF16), sb("onesb", [P, P], BF16)
        scale, gate = sb("scale", [P, 1]), sb("gate", [P, E])
        gate_b = sb("gate_b", [P, E])
        stats, mv = o_sb[:, 256:256 + NT * 6].rearrange("p (t s) -> p t s", s=6), sb("mv", [P, NT, 2])
        rs, rr, rt = sb("rs", [P, NT]), sb("rr", [P, NT]), sb("rt", [P, NT])
        sq, va = sb("sq", [P, NT]), sb("va", [P, NT])
        b2_parts, b2_raw = sb("b2_parts", [P, 3, E * D // P], BF16), sb("b2_raw", [P, E * D // P])
        wts = sb("wts", [P, 2, NT])
        index = sb("index", [P, 2, NT], U32)
        expert = sb("expert", [1, NF], I32)

        bank = ctx.enter_context(nc.psum_tensor("bank", [P, 8, 512], F32))
        ST_BANK, S_BANK, PV_BANK, RING_BANK = (0, 1), (2, 3), 4, (5, 6, 7)
        LOGIT_BANK, RANK_BANK = S_BANK

        X_AT, Y_AT = slice(0, P), slice(P, 2 * P)

        NE = NT * E
        lg, oh1, oh2, sc1, sc2, posb = (t[:, n, :] for t in (glu, lin, tanh_g) for n in range(2))
        tot, inc, cmpj = (actsT[:, 0:NE], actsT[:, NE:2 * NE], acts[:, 0:NE])
        cbf = acts[:, NE:NE + NE // 2].bitcast(BF16)
        small = slot[:, :, :].rearrange("p a b -> p (a b)")
        desc, jot, onef, v1, v2, nte, cn, e2, p1, idf = (small[:, NT * n:NT * (n + 1)] for n in range(10))
        desc = desc[:, 0:E]
        tio = small[:, NT * 10:NT * 10 + NF]
        ecmp = probs[:, 1, 2, 0:NF * E]
        esum, start8 = o_sb[:, 0:NF], o_sb[:, P:P + E]
        xnT = probs[:, 0, :, :].rearrange("p a b -> p (a b)")
        zero = probs[:, 1, 0:2, :].rearrange("p a b -> p (a b)")[:, 0:NF * D // 4]

        def cbuf(n):
            return xall[:, NQ * n:NQ * (n + 1), :]
        third = sb("third", [P, 2, NQ, D])
        y_in = [[cbuf(0), cbuf(1)], [cbuf(2), cbuf(3)], [third[:, 0, :, :], third[:, 1, :, :]]]
        x_c, xn_c, s_c, t_c = cbuf(4), cbuf(5), cbuf(6), cbuf(7)

        def dram(name, shape, dt=F32):
            return nc.dram_tensor(name, shape, dt).ap()
        xnT_d = dram("xnT_d", (P, B * S))
        xn_d = dram("xn_d", (B * S, D))
        s_d = dram("s_d", (B * S, D))
        sorted_d = dram("sorted_d", (NF * P, D))
        y_d = dram("y_d", (NF * P, D))
        parts_d = dram("parts_d", (2, 2, 3, DH, H * S), BF16)
        m_d = dram("m_d", (2, 3, HALF * S), BF16)
        b2_d = dram("b2_d", (3, E * D), BF16)

        small_in, big_in = sem("small_in"), sem("big_in")
        ident_made, consts_made, stacks_made = sem("ident_made"), sem("consts_made"), [sem("stacks_made0"), sem("stacks_made1")]
        zeroed, zero_rows, xn_out, xnT_out, bias_out, bias_in = (sem(n) for n in (
            "zeroed", "zero_rows", "xn_out", "xnT_out", "bias_out", "bias_in"))
        scattered, routed, rows_scaled, weights_made, weights_chosen = (sem(n) for n in (
            "scattered", "routed", "rows_scaled", "weights_made", "weights_chosen"))
        x_in = [sem(f"x_in{n}") for n in range(B)]
        r_dve, sq_done, xnT_copied, e2_done = sem("r_dve"), sem("sq_done"), sem("xnT_copied"), sem("e2_done")
        xnT_ready, logits_ready, ranks_ready = sem("xnT_ready"), sem("logits_ready"), sem("ranks_ready")
        rows_ready = sem("rows_ready")
        st_ready, exp_done, s_ready, max_done = (sem(n) for n in ("st_ready", "exp_done", "s_ready", "max_done"))
        selected, pv_done, o_copied, acts_done = (sem(n) for n in ("selected", "pv_done", "o_copied", "acts_done"))
        recip_done, pv_zeroed = sem("recip_done"), sem("pv_zeroed")
        split_done, m_written = sem("split_done"), [sem(f"m_written{n}") for n in range(2)]
        m_in = [sem(f"m_in{n}") for n in range(2)]
        stack_in = [[sem(f"stack{par}_in{half}") for half in range(2)] for par in range(2)]
        xq_in, xv_in = sem("xq_in"), sem("xv_in")
        roped, qk_sum, hi_done, rest_done, mid_done, low_done, parts_out = (sem(n) for n in (
            "roped", "qk_sum", "hi_done", "rest_done", "mid_done", "low_done", "parts_out"))
        ready = {n: sem(f"{n}_ready") for n in RING}
        mT_copied, v_copied, aT_copied, s_copied, s_out = (sem(n) for n in (
            "mT_copied", "v_copied", "aT_copied", "s_copied", "s_out"))
        xs_in = [sem(f"xs_in{n}") for n in range(XBUF)]
        y_out = [sem(f"y_out{n}") for n in range(FBUF)]
        slot_copied, halves_read, tanh_done, prod_done, hid_done, lin_biased = (sem(n) for n in (
            "slot_copied", "halves_read", "tanh_done", "prod_done", "hid_done", "lin_biased"))
        c_in, s_in, mix_step, mix_tanh, out_done = (sem(n) for n in ("c_in", "s_in", "mix_step", "mix_tanh", "out_done"))
        gathered = [sem(f"gathered{n}") for n in range(YBUF)]

        reader = {"Q": (roped, 1), "V": (v_copied, 1), "F": (slot_copied, 1), "H": (halves_read, 2),
                  "OT": (acts_done, 1), "mT": (mT_copied, 1), "AT": (aT_copied, 1), "WO": (s_copied, 1)}

        def ring_bank(user):
            return bank[:, RING_BANK[RING_AT[user] % 3], :]

        def st_bank(b, k):
            return bank[:, k % 4 if b == B - 1 else ST_BANK[k % 2], :]

        def st_units(b, k):
            return b * STEPS + k + 1

        block = ctx.enter_context(nc.Block())

        @block.sync
        def _(sp):
            x_rows = x_h.rearrange("(b t p) d -> b p t d", p=P, t=NQ)
            xn_rows = xn_d.rearrange("(b t p) d -> b p t d", p=P, t=NQ)
            s_rows = s_d.rearrange("(b t p) d -> b p t d", p=P, t=NQ)
            out_rows = out_h.rearrange("(b t p) d -> b p t d", p=P, t=NQ)
            for b in range(B):
                sp.dma_start(xall[:, NQ * b:NQ * (b + 1), :], x_rows[b]).then_inc(x_in[b], 16)
            for dst, src in ((wq[:, :], wq_h), (scale[:, :], scale_h), (gate[:, :], gate_w_h), (cos[:, :], cos_h),
                             (sin[:, :], sin_h),
                             (gate_b[:, :], gate_b_h.partition_broadcast(P).rearrange("p a e -> p (a e)")),
                             (wv[:, :], wv_h), (wo[:, :], wo_h), (b1, b1_h.rearrange("p (e n) -> p e n", e=E)), (b2_raw[:, :], b2_h)):
                sp.dma_start(dst, src).then_inc(small_in, 16)
            sp.wait_ge(zeroed, 1)
            z_d = sorted_d.rearrange("(p q r) d -> q p (r d)", p=P, q=4)
            for q in range(4):
                sp.dma_start(z_d[q], zero).then_inc(zero_rows, 16)
            for b in range(B):
                sp.wait_ge(rows_ready, NQ * (b + 1))
                sp.dma_start(xn_rows[b], xall[:, NQ * b:NQ * (b + 1), :]).then_inc(xn_out, 16)
            for b in range(B):
                sp.wait_ge(xnT_copied, b + 1)
                sp.dma_start(xnT_d[:, b * S:(b + 1) * S], xnT[:, b * S:(b + 1) * S]).then_inc(xnT_out, 16)

            for i, k, events in steps():
                for name, a in events:
                    if name == "xv":
                        if a == 0:
                            sp.wait_ge(xnT_out, 16 * B)
                        sp.wait_ge(ready["Q"], NTH["Q", (min(a + 1, B - 1), 3)])
                        sp.dma_start(xp[:, :], xnT_d[:, a * S:(a + 1) * S]).then_inc(xv_in, 16)
                    elif name == "xq":
                        sp.wait_ge(ready["V"], NTH["V", a - 2])
                        sp.dma_start(xp[:, :], xnT_d[:, a * S:(a + 1) * S]).then_inc(xq_in, 16)
                    elif name == "mout":
                        b, f = a
                        sp.wait_ge(mT_copied, NTH["mT", a])
                        atleast(sp, m_in[f], 16 * b)
                        sp.dma_start(m_d[f].rearrange("c (h q) -> (c h) q", h=HALF), mT[:, f, :]).then_inc(m_written[f], 16)
                    elif name == "min":
                        b, f = a
                        sp.wait_ge(m_written[f], 16 * (b + 1))
                        if b < 2:
                            sp.wait_ge(stacks_made[b], STACK_SETS[b])
                        sp.dma_start(qs[b % 2][MROW:MROW + 3, f * HALF:(f + 1) * HALF, :], m_d[f]).then_inc(m_in[f], 16)
                    elif name == "parts":
                        sp.wait_ge(low_done, NTH["low", a])
                        for half in range(2):
                            atleast(sp, stack_in[a % 2][half], STACK_LOADS * 16 * (a // 2))
                        sp.dma_start(parts_d[a % 2].rearrange("a c d (h q) -> (d h) (a c) q", h=H),
                                     parts[:, :, :, :].rearrange("p a c q -> p (a c) q")).then_inc(parts_out, 16)
                    elif name == "stack":
                        b, half = a
                        sp.wait_ge(parts_out, 16 * (b + 1))
                        if b < 2:
                            sp.wait_ge(stacks_made[b], STACK_SETS[b])
                        else:
                            sp.wait_ge(st_ready, st_units(b - 2, STEPS // 2 * (half + 1) - 1))
                        src, h0 = parts_d[b % 2], half * HALF
                        loads = [(qs, 0, 0, 0, 3), (qs, 24, 0, 0, 2), (qs, 40, 0, 0, 1)]
                        loads += [(ks, DH * r, 1, part, 1) for r, part in enumerate(K_PART)]
                        assert len(loads) == STACK_LOADS
                        for t, row, qk_at, lo, n in loads:
                            sp.dma_start(t[b % 2][row:row + DH * n, h0:h0 + HALF, :],
                                         src[qk_at, lo:lo + n, :, h0 * S:(h0 + HALF) * S].rearrange("c d x -> (c d) x")
                                         ).then_inc(stack_in[b % 2][half], 16)
                    elif name == "wload":
                        sp.dma_start(w1, w1_h.rearrange("p (e n) -> p e n", e=E)).then_inc(big_in, 16)
                        sp.dma_start(weights[:, :, W2_AT:W2_AT + 2 * D], w2_h.rearrange("p (e n) -> p e n", e=E)).then_inc(big_in, 16)
                    elif name == "bload":
                        sp.wait_ge(weights_made, 1)
                        sp.dma_start(b2_d.rearrange("c (p j) -> p c j", p=P), b2_parts[:, :, :]).then_inc(bias_out, 16)
                        sp.wait_ge(bias_out, 16)
                        sp.wait_ge(stacks_made[1], STACK_SETS[1])
                        sp.dma_start(b2[0:3, :, :], b2_d.rearrange("c (e n) -> c e n", e=E)).then_inc(bias_in, 16)
                    elif name == "xload":
                        if a == 0:
                            sp.wait_ge(scattered, 16 * 2 * NT)
                        atleast(sp, ready["F"], a - XBUF + 1)
                        sp.dma_start(xs[:, a % XBUF, :], sorted_d[a * P:(a + 1) * P, :]).then_inc(xs_in[a % XBUF], 16)
                    elif name == "yout":
                        sp.wait_ge(slot_copied, a + 1)
                        sp.dma_start(y_d[(a - LAG) * P:(a - LAG + 1) * P, :], slot[:, a % FBUF, Y_AT]).then_inc(y_out[a % FBUF], 16)
                    elif name == "WO" and a < B - 1:
                        sp.wait_ge(s_copied, a + 1)
                        sp.dma_start(s_rows[a], s_sb[:, :].rearrange("p (t d) -> p t d", t=NQ)).then_inc(s_out, 16)
                    elif name == "cload":
                        atleast(sp, mix_step, MIX * a)
                        sp.dma_start(x_c, x_rows[a]).then_inc(c_in, 16)
                        sp.dma_start(xn_c, xn_rows[a]).then_inc(c_in, 16)
                    elif name == "sload":
                        atleast(sp, mix_step, MIX * a)
                        sp.wait_ge(s_out, 16 * (a + 1))
                        sp.dma_start(s_c, s_rows[a]).then_inc(s_in, 16)
                    elif name == "out":
                        sp.wait_ge(mix_step, MIX * (a + 1))
                        sp.dma_start(out_rows[a], t_c).then_inc(out_done, 16)
            sp.wait_ge(out_done, 16 * B)
            sp.wait_ge(xn_out, 16 * B)
            for s in range(FBUF):
                sp.wait_ge(y_out[s], 16 * NF // FBUF)

        @block.gpsimd
        def _(pool):
            n_made = [0]

            def made(ins):
                n_made[0] += 1
                ins.then_inc(consts_made, 1)
                return n_made[0]

            nc.gpsimd.memset(ident[:, :], 0.0).then_inc(ident_made, 1)
            pool.wait_ge(ident_made, 1)
            nc.gpsimd.affine_select(out=ident[:, :], in_=ident[:, :], compare_op=ALU.not_equal, fill=1.0,
                                    base=0, pattern=[[-1, P]], channel_multiplier=1).then_inc(ident_made, 1)
            nc.gpsimd.memset(zero, 0.0).then_inc(zeroed, 1)
            made(nc.gpsimd.memset(mask2[:, :, :], 0.0))
            made(nc.gpsimd.memset(ltri[:, :], 1.0))
            made(nc.gpsimd.memset(onesb[:, :], 1.0))
            b = made(nc.gpsimd.memset(ones3[:, :], 0.0))
            pool.wait_ge(consts_made, b)
            b = made(nc.gpsimd.memset(ones3[0:3, :], 1.0))
            pool.wait_ge(consts_made, b)
            made(nc.gpsimd.affine_select(out=mask2[:, :, :], in_=mask2[:, :, :], compare_op=ALU.is_ge, fill=MASKED,
                                         base=0, pattern=[[0, 2], [-1, P]], channel_multiplier=1))
            made(nc.gpsimd.affine_select(out=ltri[:, :], in_=ltri[:, :], compare_op=ALU.is_gt, fill=0.0,
                                         base=0, pattern=[[1, P]], channel_multiplier=-1))
            pool.wait_ge(ident_made, 2)
            made(nc.gpsimd.tensor_copy(identb[:, :], ident[:, :]))
            made(nc.gpsimd.iota(desc, pattern=[[-1, E]], base=E, channel_multiplier=0, allow_small_or_imprecise_dtypes=True))
            made(nc.gpsimd.iota(jot, pattern=[[P, NT]], base=0, channel_multiplier=0, allow_small_or_imprecise_dtypes=True))
            made(nc.gpsimd.iota(tio, pattern=[[1, NF]], base=0, channel_multiplier=0, allow_small_or_imprecise_dtypes=True))
            made(nc.gpsimd.memset(onef, 1.0))
            assert n_made[0] == CONSTS
            for t in (ks[0], qs[0]):
                nc.gpsimd.memset(t[:, :, :].bitcast(F32), 0.0).then_inc(stacks_made[0], 1)
            pool.wait_ge(stacks_made[0], 2)
            nc.gpsimd.memset(ks[0][MROW:P, :, :], 1.0).then_inc(stacks_made[0], 1)
            pool.wait_ge(stacks_made[0], STACK_SETS[0])

            for i, k, events in steps():
                for name, a in events:
                    if name == "sel":
                        b, j = a
                        pool.wait_ge(exp_done, st_units(b, UNITS * (j + 1) - 1))
                        h0 = 2 * j % HG
                        heads = probs[:, j // 2 % 2, h0:h0 + 2, :]
                        for blk in (every_512(heads[:, 0, :]), every_512(heads[:, 1, :]), heads[:, :, PT_AT[1]:PT_AT[1] + P]):
                            nc.gpsimd.affine_select(out=blk, in_=blk, compare_op=ALU.is_ge, fill=0.0, base=0,
                                                    pattern=[[0, blk.shape[1]], [1, P]],
                                                    channel_multiplier=-1).then_inc(selected, 1)
                    elif name == "sum" and a not in CUT_BY_DVE:
                        pool.wait_ge(roped, NTH["Q", (a, 3)])
                        nc.gpsimd.tensor_tensor(qk[:, :, :], qk[:, :, :], qk_sin[:, :, :], ALU.add).then_inc(qk_sum, 1)
                    elif name == "rest" and a not in CUT_BY_DVE:
                        pool.wait_ge(hi_done, NTH["hi", a])
                        nc.gpsimd.tensor_tensor(qk[:, :, :], qk[:, :, :], parts[:, :, 0, :], ALU.subtract).then_inc(rest_done, 1)
                    elif name == "low" and a not in CUT_BY_DVE:
                        pool.wait_ge(mid_done, NTH["mid", a])
                        nc.gpsimd.tensor_tensor(parts[:, :, 2, :], qk[:, :, :], parts[:, :, 1, :], ALU.subtract).then_inc(low_done, 1)
                    elif name == "clear":
                        for t in (ks[1], qs[1]):
                            nc.gpsimd.memset(t[:, :, :].bitcast(F32), 0.0).then_inc(stacks_made[1], 1)
                        nc.gpsimd.memset(vs[:, :, :, :], 0.0).then_inc(stacks_made[1], 1)
                        nc.gpsimd.memset(weights[:, :, B2_AT:B1_AT], 0.0).then_inc(stacks_made[1], 1)
                        pool.wait_ge(stacks_made[1], 4)
                        nc.gpsimd.memset(ks[1][MROW:P, :, :], 1.0).then_inc(stacks_made[1], 1)
                        pool.wait_ge(stacks_made[1], 5)
                        nc.gpsimd.memset(vs[:, :, :, DH:DH + 1], 1.0).then_inc(stacks_made[1], 1)
                    elif name == "lift":
                        pool.wait_ge(halves_read, 2 * (a + 1))
                        for c in range(2):
                            at = slice(P * c, P * (c + 1))
                            nc.gpsimd.tensor_scalar(lin[:, a % HBUF, at], lin[:, a % HBUF, at],
                                                    chosen[:, a % WBUF, LIN_B + c:LIN_B + c + 1], None,
                                                    ALU.add).then_inc(lin_biased, 1)
                        pool.wait_ge(lin_biased, 2 * (a + 1))
                        nc.gpsimd.tensor_tensor(lin[:, a % HBUF, :], lin[:, a % HBUF, :], glu[:, a % HBUF, :],
                                                ALU.mult).then_inc(prod_done, 1)
                    elif name == "scatter":
                        if a == 0:
                            pool.wait_ge(routed, 1)
                            pool.wait_ge(zero_rows, 64)
                        s, t = a % 2, a // 2
                        pool.wait_ge(rows_scaled, t + 1)
                        nc.gpsimd.indirect_dma_start(
                            out=sorted_d, out_offset=bass.IndirectOffsetOnAxis(ap=index[:, s, t:t + 1], axis=0),
                            in_=xall[:, t, :], in_offset=None).then_inc(scattered, 16)
                    elif name == "gather":
                        c, r = a
                        if c == 0 and r == 0:
                            pool.wait_ge(scattered, 16 * 2 * NT)
                            for s in range(FBUF):
                                pool.wait_ge(y_out[s], 16 * NF // FBUF)
                        if r == 0 and c >= YBUF:
                            pool.wait_ge(mix_step, MIX * (c - YBUF + 1))
                        s, t = r // NQ, r % NQ
                        nc.gpsimd.indirect_dma_start(
                            out=y_in[c % YBUF][s][:, t, :], out_offset=None, in_=y_d,
                            in_offset=bass.IndirectOffsetOnAxis(ap=index[:, s, NQ * c + t:NQ * c + t + 1], axis=0)
                            ).then_inc(gathered[c % YBUF], 16)

        @block.scalar
        def _(act):
            act.wait_ge(r_dve, R_VAR)
            nc.scalar.activation(sq[:, :], va[:, :], ACT.Sqrt).then_inc(sq_done, 1)
            for b in range(B):
                act.wait_ge(xnT_ready, b + 1)
                nc.scalar.copy(xnT[:, b * S:(b + 1) * S], bank[:, b % 4, :]).then_inc(xnT_copied, 1)
                if b == 3:
                    act.wait_ge(r_dve, R_MS)
                    nc.scalar.activation(sq[:, :], va[:, :], ACT.Sqrt).then_inc(sq_done, 1)

            def exponentials(b, k):
                u, j = k % UNITS, k // UNITS
                g, h0 = j // 2, 2 * j % HG
                act.wait_ge(st_ready, st_units(b, k))
                if b == 0 and k == 0:
                    act.wait_ge(xnT_out, 16 * B)
                    act.wait_ge(zero_rows, 64)
                if j % 2 == 0 and u == 0 and (b > 0 or g >= 2):
                    act.wait_ge(pv_done, NTH["pv", (b - (g < 2), (g - 2) % NG, NQ - 1)])
                pt = probs[:, g % 2, :, :]
                src = st_bank(b, k)
                if u == 4:
                    dst = pt[:, h0:h0 + 2, PT_AT[2]:PT_AT[2] + 256]
                    src = src.rearrange("p (h q) -> p h q", h=2)
                else:
                    lo = 512 * (u % 2)
                    dst = pt[:, h0 + u // 2, lo:lo + 512]
                nc.scalar.activation(dst, src, ACT.Exp, scale=float(DH) ** -0.5).then_inc(exp_done, 1)

            for i, k, events in steps():
                if 0 <= i < B:
                    exponentials(i, k)
                for name, a in events:
                    if name == "oc":
                        b, g = a
                        act.wait_ge(pv_done, NTH["pv", (b, g, NQ - 1)])
                        atleast(act, ready["OT"], NTH["oc", a] - 1)
                        nc.scalar.copy(o_sb[:, :], bank[:, PV_BANK, :]).then_inc(o_copied, 1)
                    elif name == "V":
                        act.wait_ge(ready["V"], NTH["V", a])
                        if a == 0:
                            act.wait_ge(stacks_made[1], STACK_SETS[1])
                        else:
                            act.wait_ge(pv_done, NTH["pv", (a - 1, NG - 1, NQ - 1)])
                        nc.scalar.copy(vs[:, :, :, 0:DH], ring_bank((name, a)).rearrange("p (k h d) -> p k h d", k=NQ, h=H)
                                       ).then_inc(v_copied, 1)
                    elif name == "mT":
                        b, f = a
                        act.wait_ge(ready["mT"], NTH["mT", a])
                        atleast(act, m_written[f], 16 * b)
                        nc.scalar.copy(mT[:, f, :], ring_bank((name, a))[0:3 * HALF, 0:256].bitcast(BF16)).then_inc(mT_copied, 1)
                    elif name == "hi":
                        act.wait_ge(qk_sum, NTH["sum", a])
                        atleast(act, parts_out, 16 * a)
                        nc.scalar.copy(parts[:, :, 0, :], qk[:, :, :]).then_inc(hi_done, 1)
                    elif name == "mid":
                        act.wait_ge(rest_done, NTH["rest", a])
                        nc.scalar.copy(parts[:, :, 1, :], qk[:, :, :]).then_inc(mid_done, 1)
                    elif name == "rowt":
                        act.wait_ge(r_dve, R_RR)
                        act.wait_ge(xn_out, 16 * B)
                        for t in range(NT):
                            nc.scalar.mul(xall[:, t, :], xall[:, t, :], rr[:, t:t + 1]).then_inc(rows_scaled, 1)
                    elif name == "e2":
                        act.wait_ge(r_dve, R_TOP)
                        nc.scalar.activation(e2, e2, ACT.Exp).then_inc(e2_done, 1)
                    elif name == "AT":
                        act.wait_ge(ready["AT"], NTH["AT", a])
                        atleast(act, ready["WO"], a)
                        nc.scalar.copy(actsT[:, :], ring_bank((name, a))).then_inc(aT_copied, 1)
                    elif name == "WO" and a < B - 1:
                        act.wait_ge(ready["WO"], NTH["WO", a])
                        nc.scalar.copy(s_sb[:, :], ring_bank((name, a))).then_inc(s_copied, 1)
                    elif name == "wcopy":
                        if a == 0:
                            act.wait_ge(routed, 1)
                            act.wait_ge(weights_made, 1)
                            act.wait_ge(bias_in, 16)
                            act.wait_ge(scattered, 16 * 2 * NT)
                        if a >= WBUF:
                            act.wait_ge(ready["F"], a)
                        e = act.value_load(expert[0:1, a:a + 1], min_val=0, max_val=E - 1)
                        src = weights[:, :, :].rearrange("p e n -> p (e n)")[:, bass.ds(e * W_COLS, W_COLS)]
                        nc.scalar.copy(chosen[:, a % WBUF, :], src).then_inc(weights_chosen, 1)
                    elif name == "F":
                        act.wait_ge(ready["F"], a + 1)
                        if a - FBUF >= LAG:
                            act.wait_ge(y_out[a % FBUF], 16 * youts(a - FBUF))
                        cols = slot_columns(a)
                        nc.scalar.copy(slot[:, a % FBUF, cols], ring_bank((name, a))[:, cols]).then_inc(slot_copied, 1)
                    elif name == "tanh":
                        act.wait_ge(halves_read, 2 * a + 1)
                        atleast(act, hid_done, a - HBUF + 1)
                        nc.scalar.activation(tanh_g[:, a % HBUF, :], glu[:, a % HBUF, :], ACT.Tanh, scale=ALPHA / 2).then_inc(tanh_done, 1)
                    elif name == "mtanh":
                        act.wait_ge(mix_step, MIX * a + 4)
                        nc.scalar.activation(y_in[a % YBUF][1], y_in[a % YBUF][0], ACT.Tanh, scale=0.5).then_inc(mix_tanh, 1)

        @block.vector
        def _(dve):
            n_r = [0]

            def link(ins):
                n_r[0] += 1
                ins.then_inc(r_dve, 1)
                dve.wait_ge(r_dve, n_r[0])

            v = nc.vector
            for t in range(NT):
                if t % NQ == 0:
                    dve.wait_ge(x_in[t // NQ], 16)
                ins = v.bn_stats(stats[:, t, :], xall[:, t, :])
            link(ins)
            for t in range(NT):
                ins = v.bn_aggr(mv[:, t, :], stats[:, t, :])
            link(ins)
            link(v.tensor_scalar(va[:, :], mv[:, :, 1], EPS, None, ALU.add))
            assert n_r[0] == R_VAR

            def rsqrt(dst, n_act):
                dve.wait_ge(sq_done, n_act)
                link(v.reciprocal(dst, sq[:, :]))
                link(v.tensor_tensor(rt[:, :], dst, dst, ALU.mult))
                link(v.tensor_tensor(rt[:, :], rt[:, :], va[:, :], ALU.mult))
                link(v.tensor_scalar(rt[:, :], rt[:, :], -0.5, 1.5, ALU.mult, ALU.add))
                link(v.tensor_tensor(dst, dst, rt[:, :], ALU.mult))
            rsqrt(rs[:, :], 1)
            link(v.tensor_tensor(rt[:, :], rs[:, :], rs[:, :], ALU.mult))
            link(v.tensor_tensor(rt[:, :], rt[:, :], mv[:, :, 1], ALU.mult))
            link(v.tensor_scalar(va[:, :], rt[:, :], EPS, None, ALU.add))
            assert n_r[0] == R_MS
            for t in range(NT):
                v.tensor_scalar(xall[:, t, :], xall[:, t, :], mv[:, t, 0:1], rs[:, t:t + 1],
                                ALU.subtract, ALU.mult).then_inc(rows_ready, 1)
            v.memset(bank[:, PV_BANK, :], 0.0).then_inc(pv_zeroed, 1)
            dve.wait_ge(small_in, 16 * SMALL_LOADS)
            link(v.tensor_scalar(gate[:, :], gate[:, :], scale[:, 0:1], None, ALU.mult))
            assert n_r[0] == R_GATE
            rsqrt(rr[:, :], 2)
            assert n_r[0] == R_RR

            def te(ap):
                return ap.rearrange("p (t e) -> p t e", e=E)

            def et(ap):
                return ap.rearrange("p (e t) -> p e t", e=E)

            def over_e(ap):
                return ap.unsqueeze(2).to_broadcast([P, NT, E])

            def over_t(ap):
                return ap.unsqueeze(1).to_broadcast([P, NT, E])

            def top(vm, oh):
                link(v.tensor_reduce(vm, te(lg), AX.X, ALU.max))
                link(v.tensor_tensor(te(sc1), te(lg), over_e(vm), ALU.is_ge))
                link(v.tensor_tensor(te(sc1), te(sc1), over_t(desc), ALU.mult))
                link(v.tensor_reduce(idf, te(sc1), AX.X, ALU.max))
                link(v.tensor_tensor(te(oh), over_t(desc), over_e(idf), ALU.is_equal))

            def route():
                dve.wait_ge(logits_ready, 1)
                dve.wait_ge(consts_made, CONSTS)
                link(v.tensor_tensor(te(lg), te(bank[:, LOGIT_BANK, 0:NE]), over_e(rr[:, :]), ALU.mult))
                link(v.tensor_tensor(te(lg), te(lg), over_t(gate_b[:, :]), ALU.add))
                top(v1, oh1)
                link(v.scalar_tensor_tensor(te(lg), te(oh1), MASKED, te(lg), ALU.mult, ALU.add))
                top(v2, oh2)
                link(v.tensor_tensor(cbf, oh1, oh2, ALU.add))
                assert n_r[0] == R_CNT
                link(v.tensor_tensor(e2, v2, v1, ALU.subtract))
                assert n_r[0] == R_TOP
                dve.wait_ge(ranks_ready, 1)
                link(v.tensor_copy(et(tot), bank[:, RANK_BANK, NE:2 * NE].rearrange("p (t e) -> p e t", e=E)))
                for e in range(E):
                    ins = v.tensor_tensor_scan(et(inc)[:, e, :], onef, et(tot)[:, e, :], 0.0, ALU.mult, ALU.add)
                link(ins)
                link(v.tensor_tensor(et(cmpj), et(inc)[:, :, NT - 1:NT].to_broadcast([P, E, NT]),
                                     jot.unsqueeze(1).to_broadcast([P, E, NT]), ALU.is_gt))
                link(v.tensor_reduce(nte[:, 0:E], et(cmpj), AX.X, ALU.add))
                link(v.tensor_tensor_scan(cn[:, 0:E], onef[:, 0:E], nte[:, 0:E], 0.0, ALU.mult, ALU.add))
                link(v.tensor_tensor(start8, cn[:, 0:E], nte[:, 0:E], ALU.subtract))
                link(v.tensor_tensor(et(inc), et(inc), et(tot), ALU.subtract))
                link(v.tensor_tensor(te(posb), te(bank[:, RANK_BANK, 0:NE]), et(inc).rearrange("p e t -> p t e"), ALU.add))
                link(v.scalar_tensor_tensor(te(posb), over_t(start8), float(P), te(posb), ALU.mult, ALU.add))
                for s, oh in enumerate((oh1, oh2)):
                    link(v.tensor_tensor(sc2, oh, posb, ALU.mult))
                    link(v.tensor_reduce(idf, te(sc2), AX.X, ALU.add))
                    link(v.tensor_copy(index[:, s, :], idf))
                e_cmp = ecmp[0:1, :].rearrange("p (t e) -> p t e", e=E)
                link(v.tensor_tensor(e_cmp, tio[0:1, :].unsqueeze(2).to_broadcast([1, NF, E]),
                                     cn[0:1, 0:E].unsqueeze(1).to_broadcast([1, NF, E]), ALU.is_ge))
                link(v.tensor_reduce(esum[0:1, :], e_cmp, AX.X, ALU.add))
                v.tensor_scalar(expert[:, :], esum[0:1, :], float(E - 1), None, ALU.min).then_inc(routed, 1)

            def row_maxima(b, k):
                u, j = k % UNITS, k // UNITS
                hd = 2 * j + u // 2
                dve.wait_ge(s_ready, st_units(b, k))
                src = bank[:, S_BANK[k % 2], :]
                if u == 4:
                    ins = v.tensor_reduce(rowmax[:, 1, 2 * j:2 * j + 2], src.rearrange("p (h k) -> p h k", h=2), AX.X, ALU.max)
                elif u % 2 == 0:
                    ins = v.tensor_reduce(rowmax[:, 3, hd:hd + 1], src, AX.X, ALU.max)
                else:
                    v.tensor_reduce(rowmax[:, 2, hd:hd + 1], src[:, 0:384], AX.X, ALU.max)
                    ins = v.tensor_reduce(rowmax[:, 0, hd:hd + 1], src[:, 384:512], AX.X, ALU.max)
                ins.then_inc(max_done, 1)

            for i, k, events in steps():
                for name, a in events:
                    if name == "msplit":
                        b, f = a
                        done = 4 * (NTH["msplit", a] - 1)
                        dve.wait_ge(max_done, st_units(b, STEPS // 2 * (f + 1) - 1))
                        if b > 0:
                            dve.wait_ge(ready["mT"], NTH["mT", (b - 1, f)])
                        mx = rowmax[:, :, f * HALF:(f + 1) * HALF]
                        nm = msplit[:, f, :, :, :]
                        v.tensor_scalar(nm[:, :, 0, :], mx, -1.0, None, ALU.mult).then_inc(split_done, 1)
                        dve.wait_ge(split_done, done + 1)
                        v.scalar_tensor_tensor(mrest[:, :, :], mx, -1.0, nm[:, :, 0, :], ALU.mult, ALU.subtract).then_inc(split_done, 1)
                        dve.wait_ge(split_done, done + 2)
                        v.tensor_copy(nm[:, :, 1, :], mrest[:, :, :]).then_inc(split_done, 1)
                        dve.wait_ge(split_done, done + 3)
                        v.tensor_tensor(nm[:, :, 2, :], mrest[:, :, :], nm[:, :, 1, :], ALU.subtract).then_inc(split_done, 1)
                    elif name == "route":
                        route()
                    elif name == "weigh":
                        dve.wait_ge(e2_done, 1)
                        link(v.tensor_scalar(p1, e2, 1.0, None, ALU.add))
                        link(v.reciprocal(p1, p1))
                        link(v.tensor_scalar(wts[:, 0, :], p1, 0.5, None, ALU.mult))
                        link(v.tensor_tensor(wts[:, 1, :], wts[:, 0, :], e2, ALU.mult))
                    elif name == "w1":
                        dve.wait_ge(big_in, 32)
                        v.tensor_scalar(w1[:, a, :], w1[:, a, :], scale[:, 0:1], None, ALU.mult)
                    elif name == "bias":
                        lin_b = b1[:, :, 2:4]
                        v.tensor_scalar(weights[:, :, LIN_HI:LIN_HI + 2], lin_b, -1.0, LIMIT, ALU.mult, ALU.add)
                        link(v.tensor_scalar(weights[:, :, LIN_B:LIN_B + 2], lin_b, 1.0, None, ALU.add))
                        link(v.tensor_scalar(weights[:, :, LIN_LO:LIN_LO + 2], lin_b, -1.0, -LIMIT, ALU.mult, ALU.add))
                        link(v.tensor_scalar(b2_raw[:, :], b2_raw[:, :], 2.0, None, ALU.mult))
                        link(v.tensor_copy(b2_parts[:, 0, :], b2_raw[:, :]))
                        link(v.tensor_tensor(b2_raw[:, :], b2_raw[:, :], b2_parts[:, 0, :], ALU.subtract))
                        link(v.tensor_copy(b2_parts[:, 1, :], b2_raw[:, :]))
                        v.tensor_tensor(b2_parts[:, 2, :], b2_raw[:, :], b2_parts[:, 1, :], ALU.subtract).then_inc(weights_made, 1)
                    elif name == "Q":
                        b, c = a
                        dve.wait_ge(ready["Q"], NTH["Q", a])
                        if c == 0:
                            atleast(dve, low_done, b)
                        dst, tab = ((qk, cos), (qk_sin, sin))[c % 2]
                        v.tensor_tensor(dst[:, c // 2, :], ring_bank((name, a)), tab[:, :], ALU.mult).then_inc(roped, 1)
                    elif name == "H2":
                        src = ring_bank(("H", a))
                        w = chosen[:, a % WBUF, :]
                        dve.wait_ge(ready["H"], a + 1)
                        for c in range(2):
                            ins = v.tensor_scalar(glu[:, a % HBUF, P * c:P * (c + 1)], src[:, P * c:P * (c + 1)],
                                                  w[:, GLU_B + c:GLU_B + c + 1], LIMIT, ALU.add, ALU.min)
                        ins.then_inc(halves_read, 1)
                        for c in range(2):
                            ins = v.tensor_scalar(lin[:, a % HBUF, P * c:P * (c + 1)], src[:, I + P * c:I + P * (c + 1)],
                                                  w[:, LIN_LO + c:LIN_LO + c + 1], w[:, LIN_HI + c:LIN_HI + c + 1],
                                                  ALU.max, ALU.min)
                        ins.then_inc(halves_read, 1)
                    elif name == "sum" and a in CUT_BY_DVE:
                        dve.wait_ge(roped, NTH["Q", (a, 3)])
                        v.tensor_tensor(qk[:, :, :], qk[:, :, :], qk_sin[:, :, :], ALU.add).then_inc(qk_sum, 1)
                    elif name == "rest" and a in CUT_BY_DVE:
                        dve.wait_ge(hi_done, NTH["hi", a])
                        v.tensor_tensor(qk[:, :, :], qk[:, :, :], parts[:, :, 0, :], ALU.subtract).then_inc(rest_done, 1)
                    elif name == "low" and a in CUT_BY_DVE:
                        dve.wait_ge(mid_done, NTH["mid", a])
                        v.tensor_tensor(parts[:, :, 2, :], qk[:, :, :], parts[:, :, 1, :], ALU.subtract).then_inc(low_done, 1)
                    elif name == "glu":
                        dve.wait_ge(tanh_done, a + 1)
                        dve.wait_ge(prod_done, a + 1)
                        v.scalar_tensor_tensor(hid[:, a % HBUF, :], tanh_g[:, a % HBUF, :], 1.0, lin[:, a % HBUF, :],
                                               ALU.add, ALU.mult).then_inc(hid_done, 1)
                    elif name == "OT":
                        b, g = a
                        dve.wait_ge(ready["OT"], NTH["OT", a])
                        atleast(dve, acts_done, NTH["OT", a] - 1)
                        o4 = ring_bank((name, a)).rearrange("p (t c r) -> p t c r", t=NQ, c=HG)
                        v.reciprocal(recip[:, :, :], o4[:, :, :, DH]).then_inc(recip_done, 1)
                        dve.wait_ge(recip_done, NTH["OT", a])
                        atleast(dve, s_out, 16 * b)
                        dst = acts[:, :].rearrange("p (t g c d) -> p t g c d", t=NQ, g=NG, c=HG)[:, :, g, :, :]
                        v.tensor_tensor(dst, o4[:, :, :, 0:DH], recip[:, :, :].unsqueeze(3).to_broadcast([P, NQ, HG, DH]),
                                        ALU.mult).then_inc(acts_done, 1)
                    elif name == "mix":
                        c, m = a
                        y1, y2 = y_in[c % YBUF]
                        if m in (0, 1):
                            wt = wts[:, m, NQ * c:NQ * (c + 1)].unsqueeze(2).to_broadcast([P, NQ, D])
                            dve.wait_ge(gathered[c % YBUF], 16 * 2 * NQ * (c // YBUF + 1))
                            ins = v.tensor_tensor((y1, y2)[m], (y1, y2)[m], wt, ALU.mult)
                        else:
                            dve.wait_ge(mix_step, MIX * c + m)
                        if m == 2:
                            ins = v.tensor_tensor(y1, y1, y2, ALU.add)
                        elif m == 3:
                            dve.wait_ge(c_in, 32 * (c + 1))
                            ins = v.tensor_tensor(y1, y1, xn_c, ALU.add)
                        elif m == 4:
                            dve.wait_ge(mix_tanh, c + 1)
                            ins = v.scalar_tensor_tensor(y1, y2, 1.0, y1, ALU.add, ALU.mult)
                        elif m == 5:
                            if c < B - 1:
                                dve.wait_ge(s_in, 16 * (c + 1))
                                s_of = s_c
                            else:
                                dve.wait_ge(ready["WO"], B)
                                s_of = ring_bank(("WO", c)).rearrange("p (t d) -> p t d", t=NQ)
                            ins = v.tensor_tensor(y1, y1, s_of, ALU.mult)
                        elif m == 6:
                            atleast(dve, out_done, 16 * c)
                            ins = v.scalar_tensor_tensor(t_c, y1, 0.5, x_c, ALU.mult, ALU.add)
                        ins.then_inc(mix_step, 1)
                if -1 <= i < B - 1:
                    row_maxima(i + 1, k)

        @block.tensor
        def _(pe):
            pe.wait_ge(ident_made, 2)
            for b in range(B):
                pe.wait_ge(rows_ready, NQ * (b + 1))
                if b >= 4:
                    pe.wait_ge(xnT_copied, b - 3)
                for t in range(NQ):
                    ins = nc.tensor.transpose(bank[:, b % 4, P * t:P * (t + 1)], xall[:, NQ * b + t, :], ident[:, :])
                ins.then_inc(xnT_ready, 1)

            def score_keys_by_queries(b, k):
                u, j, par = k % UNITS, k // UNITS, b % 2
                ha, hb = 2 * j, 2 * j + 1
                if k in (0, STEPS // 2):
                    pe.wait_ge(m_in[k // (STEPS // 2)], 16 * (b + 1))
                if b == B - 1 and k in (2, 3):
                    pe.wait_ge(max_done, st_units(b, STEPS - 1))
                else:
                    atleast(pe, exp_done, st_units(b, k) - (4 if b == B - 1 and k >= 4 else 2))
                out = st_bank(b, k)
                todo = {0: ((ha, 0, 0),), 1: ((ha, 3, 0), (ha, 1, 128)), 2: ((hb, 0, 0),), 3: ((hb, 3, 0), (hb, 1, 128)),
                        4: ((ha, 2, 0), (hb, 2, 256))}[u]
                by_pe = b in MASKED_BY_PE
                for n, (h, kt, col) in enumerate(todo):
                    w = S - P * kt
                    ins = nc.tensor.matmul(out[:, col:col + w], ks[par][:, h, P * kt:P * (kt + 1)],
                                           qs[par][:, h, P * kt:S], start=(n == 0 or not by_pe), stop=not by_pe,
                                           skip_group_check=by_pe)
                if by_pe:
                    if u == 4:
                        dst = out.rearrange("p (h k q) -> p h k q", h=2, k=2)[:, :, 0, :]
                    else:
                        dst = out[:, 0:P * len(todo)].rearrange("p (k q) -> p k q", q=P)
                    eye = identb[:, :].unsqueeze(1).to_broadcast([P, len(todo), P])
                    ins = nc.tensor.matmul(dst, mask2[:, 0, :], eye, start=False, stop=True, skip_group_check=True)
                ins.then_inc(st_ready, 1)

            def score_queries_by_keys(b, k):
                u, j, par = k % UNITS, k // UNITS, b % 2
                ha, hb = 2 * j, 2 * j + 1
                if k in (0, STEPS // 2):
                    pe.wait_ge(stack_in[b % 2][k // (STEPS // 2)], STACK_LOADS * 16 * (b // 2 + 1))
                if b == 0 and k == 0:
                    pe.wait_ge(routed, 1)
                atleast(pe, max_done, st_units(b, k) - 2)
                out = bank[:, S_BANK[k % 2], :]
                todo = {0: ((ha, 3, 0),), 1: ((ha, 2, 0), (ha, 0, 384)), 2: ((hb, 3, 0),), 3: ((hb, 2, 0), (hb, 0, 384)),
                        4: ((ha, 1, 0), (hb, 1, 256))}[u]
                for n, (h, qt, col) in enumerate(todo):
                    w = P * (qt + 1)
                    nc.tensor.matmul(out[:, col:col + w], qs[par][0:MROW, h, P * qt:P * (qt + 1)],
                                     ks[par][0:MROW, h, 0:w], start=(n == 0), stop=False, skip_group_check=True)
                if u == 4:
                    dst, m = out.rearrange("p (h k q) -> p h k q", h=2, k=2)[:, :, 1, :], mask2[:, :, :]
                elif u % 2:
                    dst, m = out[:, 256:512].rearrange("p (k q) -> p k q", k=2), mask2[:, :, :]
                else:
                    dst, m = out[:, 384:512], mask2[:, 0, :]
                nc.tensor.matmul(dst, identb[:, :], m, start=False, stop=True, skip_group_check=True).then_inc(s_ready, 1)

            for i, k, events in steps():
                if 0 <= i < B:
                    score_keys_by_queries(i, k)
                for name, a in events:
                    if name == "logits":
                        pe.wait_ge(xnT_copied, B)
                        pe.wait_ge(r_dve, R_GATE)
                        for t in range(NT):
                            ins = nc.tensor.matmul(bank[:, LOGIT_BANK, E * t:E * (t + 1)], xnT[:, P * t:P * (t + 1)], gate[:, :],
                                                   start=True, stop=True)
                        ins.then_inc(logits_ready, 1)
                    elif name == "rank":
                        pe.wait_ge(r_dve, R_CNT)
                        nc.tensor.matmul(bank[:, RANK_BANK, 0:NE], ltri[:, :], cbf, start=True, stop=True)
                        nc.tensor.matmul(bank[:, RANK_BANK, NE:2 * NE], onesb[:, :], cbf, start=True, stop=True).then_inc(ranks_ready, 1)
                    elif name == "pv":
                        b, g, kt = a
                        if kt == 0:
                            if b in MASKED_BY_PE:
                                pe.wait_ge(exp_done, st_units(b, 2 * UNITS * (g + 1) - 1))
                            else:
                                pe.wait_ge(selected, SELECTS * NTH["sel", (b, 2 * g + 1)])
                            atleast(pe, o_copied, NTH["oc", (b, g)] - 1)
                            if g == 0:
                                pe.wait_ge(v_copied, b + 1)
                                if b == 0:
                                    pe.wait_ge(pv_zeroed, 1)
                        w = S - P * kt
                        for c in range(HG):
                            ins = nc.tensor.matmul(bank[32 * c:32 * c + VC, PV_BANK, P * kt:S], vs[:, kt, HG * g + c, :],
                                                   probs[:, g % 2, c, PT_AT[kt]:PT_AT[kt] + w],
                                                   start=(kt == 0), stop=(kt == NQ - 1), skip_group_check=True)
                        ins.then_inc(pv_done, 1)
                    elif name == "H2":
                        w, dst = chosen[:, a % WBUF, :], ring_bank(("H", a))
                        for c in range(2, 4):
                            ins = nc.tensor.matmul(dst[:, P * c:P * (c + 1)], w[:, P * c:P * (c + 1)], slot[:, a % FBUF, X_AT],
                                                   start=True, stop=True)
                        ins.then_inc(ready["H"], 1)
                    if name not in RING:
                        continue
                    if RING_AT[name, a] >= 3:
                        before = RING_USERS[RING_AT[name, a] - 3]
                        seen, signals = reader[before[0]]
                        pe.wait_ge(seen, signals * NTH[before])
                    dst = ring_bank((name, a))
                    if name == "Q":
                        b, c = a
                        if b < 2:
                            pe.wait_ge(xnT_copied, b + 1)
                            if b == 0 and c == 0:
                                pe.wait_ge(small_in, 16 * SMALL_LOADS)
                            src = xnT[:, b * S:(b + 1) * S]
                        else:
                            pe.wait_ge(xq_in, 16 * NTH["xq", b])
                            src = xp[:, :]
                        ins = nc.tensor.matmul(dst, wq[:, P * c:P * (c + 1)], src, start=True, stop=True)
                    elif name == "V":
                        pe.wait_ge(xv_in, 16 * (a + 1))
                        for t in range(NQ):
                            ins = nc.tensor.matmul(dst[:, P * t:P * (t + 1)], xp[:, P * t:P * (t + 1)], wv[:, :], start=True, stop=True)
                    elif name == "mT":
                        pe.wait_ge(split_done, 4 * NTH["msplit", a])
                        for t in range(NQ):
                            ins = nc.tensor.transpose(dst.bitcast(BF16)[0:3 * HALF, P * t:P * (t + 1)],
                                                      msplit[:, a[1], t, :, :].rearrange("p c h -> p (c h)"), identb[:, :])
                    elif name == "OT":
                        pe.wait_ge(o_copied, NTH["oc", a])
                        for t in range(NQ):
                            ins = nc.tensor.transpose(dst[:, P * t:P * (t + 1)], o_sb[:, P * t:P * (t + 1)], ident[:, :])
                    elif name == "AT":
                        pe.wait_ge(acts_done, NTH["OT", (a, NG - 1)])
                        for t in range(NQ):
                            ins = nc.tensor.transpose(dst[:, P * t:P * (t + 1)], acts[:, P * t:P * (t + 1)], ident[:, :])
                    elif name == "WO":
                        pe.wait_ge(aT_copied, a + 1)
                        for t in range(NQ):
                            ins = nc.tensor.matmul(dst[:, P * t:P * (t + 1)], actsT[:, P * t:P * (t + 1)], wo[:, :], start=True, stop=True)
                    elif name == "F":
                        if a == 0:
                            pe.wait_ge(weights_chosen, 1)
                        if a >= LAG:
                            pe.wait_ge(hid_done, a - LAG + 1)
                            w = chosen[:, (a - LAG) % WBUF, :]
                            for c in range(2):
                                nc.tensor.matmul(dst[:, Y_AT], hid[:, a % HBUF, P * c:P * (c + 1)],
                                                 w[:, W2_AT + D * c:W2_AT + D * (c + 1)], start=(c == 0), stop=False)
                            ins = nc.tensor.matmul(dst[:, Y_AT], ones3[:, :], w[:, B2_AT:B1_AT].bitcast(BF16), start=False, stop=True)
                        if a < NF:
                            pe.wait_ge(xs_in[a % XBUF], 16 * (a // XBUF + 1))
                            ins = nc.tensor.transpose(dst[:, X_AT], xs[:, a % XBUF, :], ident[:, :])
                    elif name == "H":
                        pe.wait_ge(slot_copied, a + 1)
                        pe.wait_ge(weights_chosen, a + 1)
                        w = chosen[:, a % WBUF, :]
                        for c in range(2):
                            nc.tensor.matmul(dst[:, P * c:P * (c + 1)], w[:, P * c:P * (c + 1)], slot[:, a % FBUF, X_AT],
                                             start=True, stop=True)
                        continue
                    ins.then_inc(ready[name], 1)
                if -1 <= i < B - 1:
                    score_queries_by_keys(i + 1, k)


SMALL_LOADS, STACK_LOADS = 10, 9
CONSTS, STACK_SETS = 12, (3, 6)
R_VAR, R_MS, R_GATE, R_RR, R_CNT, R_TOP = 3, 11, 12, 17, 31, 32


def slot_columns(n):
    return slice(0 if n < NF else P, P if n < LAG else 2 * P)


def youts(n):
    return len(range(n, LAG - 1, -FBUF))


def rope_tables():
    inv = (1.0 / np.float32(THETA) ** (np.arange(0, DH, 2, dtype=np.float32) / np.float32(DH))).astype(np.float32)
    f = np.arange(S, dtype=np.float32)[None, :] * inv[:, None]
    cos, sin = np.cos(f.astype(np.float64)), np.sin(f.astype(np.float64))
    cos = np.repeat(cos, 2, axis=0)
    sin = np.stack([-sin, sin], axis=1).reshape(DH, S)
    return tuple(np.ascontiguousarray(np.repeat(t, H, axis=0).astype(np.float32)) for t in (cos, sin))


def kernel(L0_attn_X, L0_attn_W_KQV, L0_attn_W_O, L0_ffn_norm_scale, L0_ffn_gate_w, L0_ffn_gate_b,
           L0_ffn_mlp1_w, L0_ffn_mlp1_b, L0_ffn_mlp2_w, L0_ffn_mlp2_b):
    import concourse.bacc as _bacc
    from concourse.bass_utils import run_bass_kernel_spmd as _run

    c = np.ascontiguousarray
    wt = np.asarray(L0_attn_W_KQV)
    order = np.array([h * DH + d for d in range(DH) for h in range(H)])
    swapped = np.array([h * DH + (d ^ 1) for d in range(DH) for h in range(H)])
    wk, wqm, wvm = wt[0:D], wt[D:2 * D], wt[2 * D:3 * D]
    wq = np.concatenate([wqm[order], wqm[swapped], wk[order], wk[swapped]], axis=0).T
    w1 = np.asarray(L0_ffn_mlp1_w).reshape(E, D, I, 2).transpose(1, 0, 3, 2).reshape(D, E * 2 * I)
    b1 = np.asarray(L0_ffn_mlp1_b).reshape(E, 2, P, 2).transpose(2, 0, 3, 1).reshape(P, E * 4)
    w2 = np.asarray(L0_ffn_mlp2_w).reshape(E, 2, P, D).transpose(2, 0, 1, 3).reshape(P, E * 2 * D)
    cos, sin = rope_tables()
    arrays = {
        "x": np.asarray(L0_attn_X).reshape(B * S, D), "wq": wq, "wv": wvm.T, "wo": np.asarray(L0_attn_W_O).T,
        "cos_t": cos, "sin_t": sin, "norm_scale": np.asarray(L0_ffn_norm_scale).reshape(D, 1),
        "gate_w": np.asarray(L0_ffn_gate_w), "gate_bias": np.asarray(L0_ffn_gate_b).reshape(1, E),
        "w1_t": w1, "b1_t": b1, "w2_t": w2, "b2_t": np.asarray(L0_ffn_mlp2_b).reshape(P, E * D // P),
    }
    arrays = {n: c(a) for n, a in arrays.items()}
    nc = _bacc.Bacc("TRN2", target_bir_lowering=False, num_devices=1)
    aps = [nc.dram_tensor("in_" + n, a.shape, mybir.dt.from_np(a.dtype), kind="ExternalInput").ap() for n, a in arrays.items()]
    out = nc.dram_tensor("out", (B * S, D), F32, kind="ExternalOutput").ap()
    build(nc, *aps, out)
    r = _run(nc, [{"in_" + n: a for n, a in arrays.items()}], core_ids=[0])
    return r.results[0]["out"].reshape(B, S, D)
```
